# Optimizing a Trainium2 kernel written in Bass

```python
import numpy as np
import jax
import jax.numpy as jnp

def _softmax(x, axis=-1):
    return jax.nn.softmax(x, axis=axis)

def _gelu(x):
    return jax.nn.gelu(x, approximate=True)

def _silu(x):
    return jax.nn.silu(x)

def _sigmoid(x):
    return jax.nn.sigmoid(x)

def _layernorm(x, axis=-1, eps=1e-05):
    m = jnp.mean(x, axis=axis, keepdims=True)
    v = jnp.var(x, axis=axis, keepdims=True)
    return (x - m) / jnp.sqrt(v + eps)

def _scatter_add(tgt, idx, src, axis=0):
    return tgt.at[idx].add(src)

def _segment_sum(src, seg, n):
    return jax.ops.segment_sum(src, seg, n)
kernel_name = 'mk_decoder_postln_d1_seqx_r4_8e2ea2'

def setup_inputs(seed: int=0):
    np.random.seed(seed)
    _w = jnp.asarray

    def _rec_inputs():
        import jax
        import jax.numpy as jnp
        _rk = jax.random.key(seed)
        x = -0.0002928 + 1 * jax.random.normal(jax.random.fold_in(_rk, 1), (32, 256, 256), jnp.float32)
        _lenS = 256 - jax.random.randint(jax.random.fold_in(_rk, 7), (32,), 0, max(1, 256 // 4) + 1, jnp.int32)
        _lenS2 = 77 - jax.random.randint(jax.random.fold_in(_rk, 8), (32,), 0, max(1, 77 // 4) + 1, jnp.int32)
        _ctx_1024P = jax.random.normal(jax.random.fold_in(_rk, 11), (32, 16, 256), jnp.float32)
        _ctx_1024c = jax.random.dirichlet(jax.random.fold_in(_rk, 511), 0.3 * jnp.ones((16,), jnp.float32), (32, 77))
        _ctx_1024t = jnp.einsum('bsk,bkd->bsd', _ctx_1024c, _ctx_1024P)
        _ctx_1024t = _ctx_1024t * jax.lax.rsqrt(jnp.mean(jnp.square(_ctx_1024t)) + 1e-12) * 0.953939
        ctx_1024 = 4.13588e-05 + 0.999923 * (_ctx_1024t + 0.3 * jax.random.normal(jax.random.fold_in(_rk, 611), (32, 77, 256), jnp.float32))
        return (x, ctx_1024)
    x, ctx_1024 = _rec_inputs()

    def _L0_attn_setup():
        import jax, jax.numpy as jnp
        import numpy as np
        N_HEADS = 16
        key = jax.random.key(seed)
        k1, k2, k3 = jax.random.split(key, 3)
        B, S, D = (2, 512, 256)
        x = jax.random.normal(k1, (B, S, D), dtype=jnp.float32)
        w_qkv = jax.random.normal(k2, (D, 3 * D), dtype=jnp.float32) * 0.02
        b_qkv = jnp.zeros((3 * D,), dtype=jnp.float32)
        w_proj = jax.random.normal(k3, (D, D), dtype=jnp.float32) * 0.02
        b_proj = jnp.zeros((D,), dtype=jnp.float32)
        return {'x': x, 'w_qkv': w_qkv, 'b_qkv': b_qkv, 'w_proj': w_proj, 'b_proj': b_proj}
    _L0_attn_all = _L0_attn_setup()
    _L0_attn_in = {k: v for k, v in _L0_attn_all.items() if k in ('w_qkv', 'b_qkv', 'w_proj', 'b_proj')}
    del _L0_attn_all

    def _L0_xattn_setup():
        import jax, jax.numpy as jnp
        import numpy as np
        HIDDEN = 256
        HEADS = 16
        HEAD_DIM = 64
        key = jax.random.key(seed)
        ks = jax.random.split(key, 7)
        B, Q, K = (2, 512, 1024)
        s = 1.0 / np.sqrt(HIDDEN)
        return {'query': jax.random.normal(ks[0], (B, Q, HIDDEN), dtype=jnp.float32), 'key': jax.random.normal(ks[1], (B, K, HIDDEN), dtype=jnp.float32), 'value': jax.random.normal(ks[2], (B, K, HIDDEN), dtype=jnp.float32), 'w_q': jax.random.normal(ks[3], (HIDDEN, HEADS * HEAD_DIM), dtype=jnp.float32) * s, 'w_k': jax.random.normal(ks[4], (HIDDEN, HEADS * HEAD_DIM), dtype=jnp.float32) * s, 'w_v': jax.random.normal(ks[5], (HIDDEN, HEADS * HEAD_DIM), dtype=jnp.float32) * s, 'w_o': jax.random.normal(ks[6], (HEADS * HEAD_DIM, HIDDEN), dtype=jnp.float32) * s}
    _L0_xattn_all = _L0_xattn_setup()
    _L0_xattn_in = {k: v for k, v in _L0_xattn_all.items() if k in ('w_q', 'w_k', 'w_v', 'w_o')}
    del _L0_xattn_all

    def _L0_ffn_setup():
        import jax, jax.numpy as jnp
        import numpy as np
        import math
        D_IN = 256
        FEATURES = (1024, 1024, 256)
        BATCH, SEQ = (8, 512)

        def _conn_dense(kernel_bool, x):
            w = jnp.where(kernel_bool, jnp.float32(1.0), jnp.float32(-1.0))
            return x @ w
        key = jax.random.key(seed)
        kx, kk0, kk1, kk2 = jax.random.split(key, 4)
        x = jax.random.normal(kx, (BATCH, SEQ, D_IN), dtype=jnp.float32)
        k0 = jax.random.randint(kk0, (2 * D_IN, FEATURES[0]), 0, 2).astype(jnp.bool_)
        k1 = jax.random.randint(kk1, (FEATURES[0], FEATURES[1]), 0, 2).astype(jnp.bool_)
        k2 = jax.random.randint(kk2, (FEATURES[1], FEATURES[2]), 0, 2).astype(jnp.bool_)
        s0 = jnp.asarray(1.0 / math.sqrt(2 * D_IN), dtype=jnp.float32)
        s1 = jnp.asarray(1.0 / math.sqrt(FEATURES[0]), dtype=jnp.float32)
        s2 = jnp.asarray(1.0 / math.sqrt(FEATURES[1]), dtype=jnp.float32)
        return {'x': x, 'k0': k0, 'k1': k1, 'k2': k2, 's0': s0, 's1': s1, 's2': s2}
    _L0_ffn_all = _L0_ffn_setup()
    _L0_ffn_in = {k: v for k, v in _L0_ffn_all.items() if k in ('k0', 'k1', 'k2', 's0', 's1', 's2')}
    del _L0_ffn_all
    return {'x': x, 'ctx_1024': ctx_1024, 'L0_attn_w_qkv': _L0_attn_in['w_qkv'], 'L0_attn_b_qkv': _L0_attn_in['b_qkv'], 'L0_attn_w_proj': _L0_attn_in['w_proj'], 'L0_attn_b_proj': _L0_attn_in['b_proj'], 'L0_xattn_w_q': _L0_xattn_in['w_q'], 'L0_xattn_w_k': _L0_xattn_in['w_k'], 'L0_xattn_w_v': _L0_xattn_in['w_v'], 'L0_xattn_w_o': _L0_xattn_in['w_o'], 'L0_ffn_k0': _L0_ffn_in['k0'], 'L0_ffn_k1': _L0_ffn_in['k1'], 'L0_ffn_k2': _L0_ffn_in['k2'], 'L0_ffn_s0': _L0_ffn_in['s0'], 'L0_ffn_s1': _L0_ffn_in['s1'], 'L0_ffn_s2': _L0_ffn_in['s2']}

def reference(x, ctx_1024, L0_attn_w_qkv, L0_attn_b_qkv, L0_attn_w_proj, L0_attn_b_proj, L0_xattn_w_q, L0_xattn_w_k, L0_xattn_w_v, L0_xattn_w_o, L0_ffn_k0, L0_ffn_k1, L0_ffn_k2, L0_ffn_s0, L0_ffn_s1, L0_ffn_s2):
    import jax
    import jax.numpy as jnp

    def _L0_attn_ref(x, w_qkv, b_qkv, w_proj, b_proj):
        import jax, jax.numpy as jnp
        import numpy as np
        N_HEADS = 16
        B, S, D = x.shape
        H = N_HEADS
        hd = D // H
        scale = 1.0 / jnp.sqrt(jnp.asarray(hd, dtype=x.dtype))
        qkv = x @ w_qkv + b_qkv
        q, k, v = jnp.split(qkv, 3, axis=-1)
        q = q.reshape(B, S, H, hd).transpose(0, 2, 1, 3)
        k = k.reshape(B, S, H, hd).transpose(0, 2, 1, 3)
        v = v.reshape(B, S, H, hd).transpose(0, 2, 1, 3)
        scores = jnp.einsum('bhqd,bhkd->bhqk', q, k) * scale
        causal = jnp.tril(jnp.ones((S, S), dtype=bool))
        scores = jnp.where(causal, scores, -jnp.inf)
        attn = jax.nn.softmax(scores, axis=-1)
        out = jnp.einsum('bhqk,bhkd->bhqd', attn, v)
        out = out.transpose(0, 2, 1, 3).reshape(B, S, D)
        return out @ w_proj + b_proj

    def _L0_xattn_ref(query, key, value, w_q, w_k, w_v, w_o):
        import jax, jax.numpy as jnp
        import numpy as np
        HIDDEN = 256
        HEADS = 16
        HEAD_DIM = 64
        B, Q, _ = query.shape
        Kl = key.shape[1]
        scale = HEAD_DIM ** (-0.5)
        q = (query @ w_q).reshape(B, Q, HEADS, HEAD_DIM).transpose(0, 2, 1, 3)
        k = (key @ w_k).reshape(B, Kl, HEADS, HEAD_DIM).transpose(0, 2, 1, 3)
        v = (value @ w_v).reshape(B, Kl, HEADS, HEAD_DIM).transpose(0, 2, 1, 3)
        scores = jnp.einsum('bhqd,bhkd->bhqk', q, k) * scale
        attn = jax.nn.softmax(scores, axis=-1)
        out = jnp.einsum('bhqk,bhkd->bhqd', attn, v)
        out = out.transpose(0, 2, 1, 3).reshape(B, Q, HEADS * HEAD_DIM)
        return out @ w_o

    def _L0_ffn_ref(x, k0, k1, k2, s0, s1, s2):
        import jax, jax.numpy as jnp
        import numpy as np
        import math
        D_IN = 256
        FEATURES = (1024, 1024, 256)
        BATCH, SEQ = (8, 512)

        def _conn_dense(kernel_bool, x):
            w = jnp.where(kernel_bool, jnp.float32(1.0), jnp.float32(-1.0))
            return x @ w
        h = jnp.concatenate([x, -x], axis=-1)
        h = s0 * _conn_dense(k0, h)
        h = jax.nn.relu(h) * 2
        h = s1 * _conn_dense(k1, h)
        h = jax.nn.relu(h) * 2
        h = s2 * _conn_dense(k2, h)
        return h
    x = _layernorm(x + _L0_attn_ref(x, L0_attn_w_qkv, L0_attn_b_qkv, L0_attn_w_proj, L0_attn_b_proj), axis=-1)
    x = _layernorm(x + _L0_xattn_ref(x, ctx_1024, ctx_1024, L0_xattn_w_q, L0_xattn_w_k, L0_xattn_w_v, L0_xattn_w_o), axis=-1)
    x = _layernorm(x + _L0_ffn_ref(x, L0_ffn_k0, L0_ffn_k1, L0_ffn_k2, L0_ffn_s0, L0_ffn_s1, L0_ffn_s2), axis=-1)
    return x

_drawn_inputs = setup_inputs


def setup_inputs(seed=0):
    import zlib

    import numpy as np

    out = dict(_drawn_inputs(seed))
    spreads = {'L0_attn_b_qkv': (0.0, 0.341), 'L0_attn_b_proj': (0.0, 0.1)}
    factors = {'L0_attn_w_qkv': 4.793}
    for name, (base, spread) in spreads.items():
        noise = np.random.default_rng([zlib.crc32(name.encode()), seed]).standard_normal(out[name].shape)
        drawn = base * np.exp(spread * noise) if base else spread * noise
        out[name] = jnp.asarray(drawn.astype(out[name].dtype))
    for name, factor in factors.items():
        out[name] = (out[name] * factor).astype(out[name].dtype)
    return out
```

```python
from contextlib import ExitStack

import concourse.bass as bass
from concourse import mybir

F32 = mybir.dt.float32
F32R = mybir.dt.float32r
F16 = mybir.dt.float16
BF16 = mybir.dt.bfloat16
U8 = mybir.dt.uint8
ALU = mybir.AluOpType
ACT = mybir.ActivationFunctionType
AX_X = mybir.AxisListType.X

P = 128
MASKED = -1e30
LOWEST = -3e38
EPS = 1e-5


def nth(i, per, k):
    return i * per + k


def decoder_layer(nc, x, ctx, w_qkv, b_qkv, w_proj, b_proj, w_q, w_k, w_v, w_o, k0, k1, k2, s0, s1, s2, out):
    B, S, D = x.shape
    SK = ctx.shape[1]
    H = 16
    HD = D // H
    XD = w_q.shape[1] // H
    F = k1.shape[0]
    KD = D // P
    TB = S // P
    NP = H // 2
    KX = w_q.shape[1] // P
    KF = F // P
    R1_SCALE = 1.0 / 16
    SELF_SCALE = float(HD) ** -0.5
    CROSS_SCALE = float(XD) ** -0.5
    ROW_M = 3 * HD
    KST = ROW_M + 1
    NQ = D // HD // 2

    with ExitStack() as stack:
        def sb(name, shape, dt):
            return stack.enter_context(nc.sbuf_tensor(name, shape, dt))

        def sem(name):
            return stack.enter_context(nc.semaphore(name))

        wqkv_h = sb("wqkv_h", [P, KD, 3 * D], F32R)
        wqkv_l = sb("wqkv_l", [P, KD, 3 * D], F32R)
        wp_h = sb("wp_h", [P, KD, D], F32R)
        wp_l = sb("wp_l", [P, KD, D], F32R)
        wq_h = sb("wq_h", [P, KD, H * XD], F32R)
        wq_l = sb("wq_l", [P, KD, H * XD], F32R)
        wk = sb("wk", [P, KD, H * XD], F32)
        wv = sb("wv", [P, KD, H * XD], F32)
        wo_h = sb("wo_h", [P, KX, D], F32R)
        wo_l = sb("wo_l", [P, KX, D], F32R)
        w0 = sb("w0", [P, KD, F], F16)
        w1 = sb("w1", [P, KF, F], F16)
        w2 = sb("w2", [P, KF, D], F16)
        bias_qk = sb("bias_qk", [P, 2 * KD], F32)
        bias_v = sb("bias_v", [P, TB, D], F32)
        bias_p = sb("bias_p", [P, TB, D], F32)
        ident = sb("ident", [P, P], F32)
        causal = sb("causal", [P, 3 * P], BF16)
        head_row = sb("head_row", [H, H, SK + 1], F32R)
        sum_col = sb("sum_col", [SK, 4, 32], F32)
        minus_half = sb("minus_half", [P, TB], F32)
        scal = sb("scal", [P, 3], F32)
        sgn = sb("sgn", [P, 2], F32)
        tmp2 = sb("tmp2", [P, 2], F32)
        ffn_coef = sb("ffn_coef", [P, 4], F32)
        x_in = sb("x_in", [P, TB, D], F32)
        xb = sb("xb", [P, TB, D], F32)
        xt_h = sb("xt_h", [P, KD, S], F32R)
        xt_l = sb("xt_l", [P, KD, S], F32R)
        low = sb("low", [P, KX, S], F32R)
        qk_h = low[:, 0:4, :]
        qk_l = low[:, 4:8, :]
        q2_l = low
        high = sb("high", [P, KX, S], F32R)
        q_st = high
        q2_h = high
        k_st = sb("k_st", [P, NP, S], F32R)
        v = sb("v", [P, TB, H, 2 * HD], F32)
        probs = sb("probs", [P, 4, 512], F32)
        pr = probs[:].rearrange("p a b -> p (a b)")[:, 0:2 * 768].rearrange("p (n a b) -> p n a b", n=2, a=2)
        arena = sb("arena", [P, KX * S], F32)
        o_raw = arena[:, 0:4 * S].rearrange("p (g t) -> p g t", g=4)
        o_c = arena[:, 4 * S:6 * S].rearrange("p (m t) -> p m t", m=KD)
        s_c = arena[:, 6 * S:8 * S].rearrange("p (m t) -> p m t", m=KD)
        inv2 = arena[:].rearrange("p (m t) -> p m t", m=KX)
        o_h = sb("o_h", [P, KD, S], F32R)
        o_l = sb("o_l", [P, KD, S], F32R)
        x1 = sb("x1", [P, TB, D], F32)
        c_in = sb("c_in", [SK, D], F32)
        ct = sb("ct", [P, KD, SK + 1], F32)
        kbd_h = sb("kbd_h", [P, KX, 2, P], F32R)
        k2_l = sb("k2_l", [P, KX, SK + 1], F32R)
        v2 = sb("v2", [SK, H * XD], F32)
        o2 = sb("o2", [P, KX, S], F32)
        inv_s = sb("inv_s", [P, S], F32)
        x2 = sb("x2", [P, TB, D], F32)
        x2t_h = sb("x2t_h", [P, KD, S], F16)
        x2t_l = sb("x2t_l", [P, KD, S], F16)
        r0_h = sb("r0_h", [P, KF, S], F16)
        r0_l = sb("r0_l", [P, KF, S], F16)
        r1_h = sb("r1_h", [P, KF, S], F16)
        r1_l = sb("r1_l", [P, KF, S], F16)
        y3 = sb("y3", [P, TB, D], F32)
        junk = sb("junk", [P, 4, 256], BF16)
        row_max = sb("row_max", [P, TB, H], F32)
        row_max2 = sb("row_max2", [P, TB, H], F32)
        neg_max = sb("neg_max", [H, S], F32R)
        neg_max2 = neg_max
        stats = sb("stats", [P, 3, TB, 6], F32)
        mv = sb("mv", [P, 3, TB, 2], F32)
        var_eps = sb("var_eps", [P, 3, TB], F32)
        rstd = sb("rstd", [P, 3, TB], F32)

        ps = stack.enter_context(nc.psum_tensor("ps", [P, 8, 512], F32))

        w_in = [sem(f"w_in{n}") for n in range(4)]
        wkv_in = sem("wkv_in")
        kb_in = sem("kb_in")
        small_in = sem("small_in")
        x_loaded = sem("x_loaded")
        c_loaded = sem("c_loaded")
        q_stacked = sem("q_stacked")
        k_stacked = sem("k_stacked")
        max_stacked = sem("max_stacked")
        o_packed = sem("o_packed")
        inv_spread = sem("inv_spread")
        stored = sem("stored")
        const_pool = sem("const_pool")
        const_dve = sem("const_dve")
        w_high = sem("w_high")
        w_low = sem("w_low")
        w_bin = sem("w_bin")
        coef = sem("coef")
        pe_xt, pe_qk, pe_v, pe_x2t, pe_ct, pe_k2, pe_v2 = (sem("pe_" + n) for n in "xt qk v x2t ct k2 v2".split())
        pe_sq, pe_mt, pe_st, pe_pv, pe_pj, pe_x1t = (sem("pe_" + n) for n in "sq mt st pv pj x1t".split())
        pe_q2, pe_sq2, pe_mt2, pe_st2, pe_pv2, pe_wo = (sem("pe_" + n) for n in "q2 sq2 mt2 st2 pv2 wo".split())
        pe_z0, pe_z1, pe_z2 = (sem("pe_" + n) for n in "z0 z1 z2".split())
        a_xt, a_qk, a_x2t, a_ct, a_k2, a_v2, a_nm, a_p, a_o, a_oh, a_x1t, a_q2, a_nm2, a_p2, a_o2, a_o2h, a_r0, a_r1 = (
            sem("a_" + n) for n in "xt qk x2t ct k2 v2 nm p o oh x1t q2 nm2 p2 o2 o2h r0 r1".split())
        d_xt, d_qk, d_v, d_x2t, d_k2, d_v2, d_mx, d_rc, d_on, d_ol, d_y1, d_x1, d_x1t, d_q2, d_mx2, d_is = (
            sem("d_" + n) for n in "xt qk v x2t k2 v2 mx rc on ol y1 x1 x1t q2 mx2 is".split())
        d_o2, d_o2l, d_y2, d_x2, d_r0, d_r1, d_y3, d_out = (
            sem("d_" + n) for n in "o2 o2l y2 x2 r0 r1 y3 out".split())
        d_bn = [sem(f"d_bn{n}") for n in range(3)]
        d_ag = [sem(f"d_ag{n}") for n in range(3)]
        g_xb, g_p = sem("g_xb"), sem("g_p")
        passed_dve, passed_pool = sem("passed_dve"), sem("passed_pool")
        g_ve = [sem(f"g_ve{n}") for n in range(3)]
        g_rs = [sem(f"g_rs{n}") for n in range(3)]

        x_rows = x.rearrange("b s d -> (b s) d")
        ctx_rows = ctx.rearrange("b s d -> (b s) d")
        out_rows = out.rearrange("b s d -> (b s) d")

        def column_pieces(n, stage, dst):
            if n:
                return [(stage, dst[:])]
            pieces = [(stage[:, :, 2 * D:], dst[:, :, 2 * D:])]
            for kk in range(KD):
                for m in range(2 * KD):
                    src = stage[:, kk, (m // 2) * D:(m // 2 + 1) * D].rearrange("p (n e d) -> p e d n", e=2, d=HD)
                    pieces.append((src[:, m % 2], dst[:, kk, m * P:(m + 1) * P].rearrange("p (d n) -> p d n", n=NP)))
            return pieces

        qk_d = nc.dram_tensor("qk_scratch", [2, P, 2 * KD, S], F32, kind="Internal").ap()
        o_d = nc.dram_tensor("o_scratch", [P, 4, S], F32, kind="Internal").ap()
        inv_d = nc.dram_tensor("inv_scratch", [P, S], F32, kind="Internal").ap()
        qk_saved, o_saved, inv_saved = sem("qk_saved"), sem("o_saved"), sem("inv_saved")

        block = stack.enter_context(nc.Block())

        kb0 = r0_h[:].rearrange("p a b -> p (a b)").bitcast(U8).rearrange("p (k n) -> p k n", k=2 * KD)
        kb2 = r0_l[:].rearrange("p a b -> p (a b)").bitcast(U8)[:, 0:KF * D].rearrange("p (k n) -> p k n", k=KF)
        kb1 = probs[:].rearrange("p a b -> p (a b)").bitcast(U8).rearrange("p (k n) -> p k n", k=KF)
        stage_qkv = arena[:, 0:KD * 3 * D].rearrange("p (k n) -> p k n", k=KD)
        stage_p = o2[:].rearrange("p a b -> p (a b)")[:, 0:KD * D].rearrange("p (k n) -> p k n", k=KD)
        stage_q = arena[:].rearrange("p (k n) -> p k n", k=KD)
        stage_o = o2[:]
        split = ((stage_qkv, wqkv_h, wqkv_l), (stage_p, wp_h, wp_l), (stage_q, wq_h, wq_l), (stage_o, wo_h, wo_l))

        @block.sync
        def _(sp):
            sp.dma_start(x_in[:], x[0].rearrange("(b p) d -> p b d", p=P)).then_inc(x_loaded, 16)
            sp.dma_start(c_in[:], ctx[0]).then_inc(c_loaded, 16)
            sp.dma_start(stage_qkv, w_qkv.rearrange("(k p) n -> p k n", p=P)).then_inc(w_in[0], 16)
            sp.dma_start(stage_p, w_proj.rearrange("(k p) n -> p k n", p=P)).then_inc(w_in[1], 16)
            for m in range(2 * KD):
                src = b_qkv[(m // 2) * D:(m // 2 + 1) * D].rearrange("(p e d) -> e d p", e=2, d=HD)[m % 2]
                sp.dma_start(bias_qk[:, m:m + 1], src, allow_slow_non_contiguous=True).then_inc(small_in, 16)
            for b in range(TB):
                sp.dma_start(bias_v[:, b, :], b_qkv[2 * D:3 * D].partition_broadcast(P)).then_inc(small_in, 16)
                sp.dma_start(bias_p[:, b, :], b_proj.partition_broadcast(P)).then_inc(small_in, 16)
            for n, s in enumerate((s0, s1, s2)):
                sp.dma_start(scal[:, n:n + 1], s.partition_broadcast(P)).then_inc(small_in, 16)
            sp.dma_start(kb0, k0.rearrange("(k p) n -> p k n", p=P)).then_inc(kb_in, 16)
            sp.dma_start(kb2, k2.rearrange("(k p) n -> p k n", p=P)).then_inc(kb_in, 16)
            sp.dma_start(kb1, k1.rearrange("(k p) n -> p k n", p=P)).then_inc(kb_in, 16)
            sp.dma_start(wk[:], w_k.rearrange("(k p) n -> p k n", p=P)).then_inc(wkv_in, 16)
            sp.dma_start(wv[:], w_v.rearrange("(k p) n -> p k n", p=P)).then_inc(wkv_in, 16)
            sp.wait_ge(w_low, 1)
            sp.dma_start(stage_q, w_q.rearrange("(k p) n -> p k n", p=P)).then_inc(w_in[2], 16)
            sp.wait_ge(w_low, 2)
            sp.dma_start(stage_o, w_o.rearrange("(k p) n -> p k n", p=P)).then_inc(w_in[3], 16)
            sp.wait_ge(w_low, 4)

            def attention(i, first, f, more=True):
                sp.wait_ge(a_qk, nth(i, 4, 4))
                if not first:
                    sp.wait_ge(q_stacked, nth(f, 64, 64))
                    sp.wait_ge(k_stacked, nth(f, 64, 64))
                sp.dma_start(qk_d[0], qk_h.bitcast(F32)).then_inc(qk_saved, 16)
                sp.wait_ge(d_qk, nth(i, 4, 4))
                sp.dma_start(qk_d[1], qk_l.bitcast(F32)).then_inc(qk_saved, 16)
                sp.wait_ge(qk_saved, nth(i, 32, 32))
                if not first:
                    sp.wait_ge(pe_wo, nth(f, 1, 1))
                    sp.wait_ge(pe_st, nth(f, 8, 8))
                for dst, at, both, one, done in ((q_st, 0, HD, 0, q_stacked), (k_st, KD, 0, 2 * HD, k_stacked)):
                    for e in range(2):
                        src = qk_d[:, :, at + e, :].rearrange("a (d p) t -> (a d) p t", p=NP)
                        r = 64 * e + both
                        sp.dma_start(dst[r:r + 2 * HD, :, :].bitcast(F32), src).then_inc(done, 16)
                        r = 64 * e + one
                        sp.dma_start(dst[r:r + HD, :, :].bitcast(F32), src[0:HD]).then_inc(done, 16)
                sp.wait_ge(a_nm, nth(i, 1, 1))
                sp.wait_ge(q_stacked, nth(i, 64, 64))
                for e in range(2):
                    sp.dma_start(q_st[64 * e + ROW_M:64 * e + ROW_M + 1, :, :].bitcast(F32),
                                 neg_max[e::2, :].bitcast(F32)).then_inc(max_stacked, 16)
                if more:
                    load_next(i)
                sp.wait_ge(a_o, nth(i, 2, 2))
                if not first:
                    sp.wait_ge(o_packed, nth(f, 64, 64))
                sp.dma_start(o_d, o_raw).then_inc(o_saved, 16)
                sp.wait_ge(o_saved, nth(i, 16, 16))
                for part, dst in ((1, s_c), (0, o_c)):
                    for e in range(2):
                        sp.dma_start(dst[64 * e:64 * e + 64, :, :],
                                     o_d[part::2, e::2, :]).then_inc(o_packed, 16)
                sp.wait_ge(d_is, nth(i, 1, 1))
                if not first:
                    sp.wait_ge(inv_spread, nth(f, 64, 64))
                sp.dma_start(inv_d, inv_s[:]).then_inc(inv_saved, 16)
                sp.wait_ge(inv_saved, nth(i, 16, 16))
                for e in range(2):
                    for b in range(2):
                        r = 32 * (2 * b + e)
                        sp.dma_start(inv2[64 * e:64 * e + 64, b::2, :],
                                     inv_d[r:r + 4, :].unsqueeze(0).broadcast_to([64, 4, S])).then_inc(inv_spread, 16)
                if not first:
                    store(f)

            def load_next(i):
                sp.wait_ge(pe_xt, nth(i, 1, 1))
                sp.wait_ge(g_xb, nth(i, 1, 1))
                sp.wait_ge(pe_ct, nth(i, 1, 1))
                sp.dma_start(x_in[:], x_rows[bass.ds((i + 1) * S, S), :].rearrange("(b p) d -> p b d", p=P))\
                  .then_inc(x_loaded, 16)
                sp.dma_start(c_in[:], ctx_rows[bass.ds((i + 1) * SK, SK), :]).then_inc(c_loaded, 16)

            def store(f):
                sp.wait_ge(d_out, nth(f, 2, 2))
                sp.dma_start(out_rows[bass.ds(f * S, S), :].rearrange("(b p) d -> p b d", p=P), y3[:])\
                  .then_inc(stored, 16)

            attention(0, True, None)
            with sp.Fori(1, B - 1) as i:
                attention(i, False, i - 1)
            attention(B - 1, False, B - 2, more=False)
            store(B - 1)
            sp.wait_ge(stored, 16 * B)

        @block.gpsimd
        def _(pool):
            pool.memset(ident[:], 0.0).then_inc(const_pool, 1)
            pool.memset(causal[:], 0.0).then_inc(const_pool, 1)
            pool.memset(head_row[:].bitcast(F32), 1.0).then_inc(const_pool, 1)
            pool.wait_ge(const_pool, 3)
            pool.affine_select(out=ident[:], in_=ident[:], compare_op=ALU.not_equal, fill=1.0, base=0,
                               pattern=[[-1, P]], channel_multiplier=1).then_inc(const_pool, 1)
            for c in (0, 2):
                tri = causal[:, c * P:(c + 1) * P]
                pool.affine_select(out=tri, in_=tri, compare_op=ALU.is_ge, fill=MASKED, base=0,
                                   pattern=[[-1, P]], channel_multiplier=1).then_inc(const_pool, 1)
            pool.affine_select(out=head_row[:], in_=head_row[:], compare_op=ALU.is_equal, fill=0.0, base=0,
                               pattern=[[-1, H], [0, SK + 1]], channel_multiplier=1).then_inc(const_pool, 1)
            pool.memset(minus_half[:], -0.5).then_inc(const_pool, 1)
            pool.memset(sum_col[:], 0.0).then_inc(const_pool, 1)
            pool.wait_ge(const_pool, 9)
            for g in range(4):
                pool.memset(sum_col[:, g, g:g + 1], 1.0).then_inc(const_pool, 1)
            pool.memset(sum_col[:, 0, 4:32], 1.0).then_inc(const_pool, 1)
            pool.wait_ge(const_pool, 14)
            pool.wait_ge(small_in, 16 * 11)

            def attention(i, first, f):
                pool.wait_ge(x_loaded, nth(i, 16, 16))
                if not first:
                    pool.wait_ge(d_y1, nth(f, 1, 1))
                pool.tensor_tensor(xb[:], x_in[:], bias_p[:], ALU.add).then_inc(g_xb, 1)
                for n in range(NP):
                    pool.wait_ge(a_p, nth(i, NP, n + 1))
                    pool.sem_inc(passed_pool, 1)
                    diag = pr[:, n % 2, :, 0:2 * P].rearrange("p a (b q) -> p a b q", b=2)
                    pool.affine_select(out=diag, in_=diag, compare_op=ALU.is_ge, fill=0.0, base=0,
                                       pattern=[[0, 2], [0, 2], [1, P]], channel_multiplier=-1).then_inc(g_p, 1)
                inverse_deviation(0, i)
                if not first:
                    inverse_deviation(2, f)
                inverse_deviation(1, i)

            def inverse_deviation(n, i):
                pool.wait_ge(d_ag[n], nth(i, 2, 2))
                pool.sem_inc(passed_pool, 1)
                pool.tensor_scalar(var_eps[:, n, :], mv[:, n, :, 1], EPS, None, ALU.add).then_inc(g_ve[n], 1)
                pool.wait_ge(g_ve[n], nth(i, 1, 1))
                pool.tensor_tensor(rstd[:, n, :], var_eps[:, n, :], minus_half[:], ALU.pow).then_inc(g_rs[n], 1)

            attention(0, True, None)
            with pool.Fori(1, B) as i:
                attention(i, False, i - 1)
            inverse_deviation(2, B - 1)

        @block.scalar
        def _(act):
            for n, (stage, high_part, _) in enumerate(split):
                act.wait_ge(w_in[n], 16)
                pieces = column_pieces(n, stage, high_part)
                for src, dst in pieces:
                    last = act.activation(dst, src, ACT.Copy)
                last.then_inc(w_high, 1)
            act.wait_ge(small_in, 16 * 11)

            def relu(z, r_h, pe_z, done, low_done, f, u):
                act.wait_ge(pe_z, nth(f, 4, u + 1))
                act.activation(r_h[:, 2 * u:2 * u + 2, :], ps[:, u % 2, :], ACT.Relu).then_inc(done, 1)

            def attention(i, first, f):
                act.wait_ge(pe_xt, nth(i, 1, 1))
                act.activation(xt_h[:], ps[:, 2, :], ACT.Copy).then_inc(a_xt, 1)
                for m in range(4):
                    act.wait_ge(pe_qk, nth(i, 2, m // 2 + 1))
                    act.activation(qk_h[:, m, :], ps[:, 3 + m // 2, (m % 2) * S:(m % 2 + 1) * S], ACT.Identity,
                                   bias=bias_qk[:, m:m + 1]).then_inc(a_qk, 1)
                if not first:
                    transposed_x2(f)
                act.wait_ge(pe_ct, nth(i, 1, 1))
                act.activation(ct[:, :, 0:SK], ps[:, 2, 0:2 * P].rearrange("p (k t) -> p k t", k=2)[:, :, 0:SK],
                               ACT.Copy).then_inc(a_ct, 1)
                for n in range(2):
                    act.wait_ge(pe_k2, nth(i, 2, n + 1))
                    src = ps[:, 6 + n, :].rearrange("p (m t) -> p m t", m=4)
                    for e in range(2):
                        act.activation(kbd_h[64 * e:64 * e + 64, 4 * n:4 * n + 4, e, 0:SK],
                                       src[64 * e:64 * e + 64, :, 0:SK], ACT.Copy).then_inc(a_k2, 1)
                act.wait_ge(pe_v2, nth(i, 2, 1))
                act.activation(v2[:, 0:512], ps[0:SK, 2, :], ACT.Copy).then_inc(a_v2, 1)
                if not first:
                    for u in range(4):
                        relu(ps, r0_h, pe_z0, a_r0, d_r0, f, u)
                    relu(ps, r1_h, pe_z1, a_r1, d_r1, f, 0)
                    relu(ps, r1_h, pe_z1, a_r1, d_r1, f, 1)
                act.wait_ge(pe_mt, nth(i, 1, 1))
                act.activation(neg_max[:], ps[0:H, 2, 0:S], ACT.Copy, scale=-1.0).then_inc(a_nm, 1)
                if not first:
                    relu(ps, r1_h, pe_z1, a_r1, d_r1, f, 2)
                for n in range(NP):
                    act.wait_ge(pe_st, nth(i, NP, n + 1))
                    if n >= 2:
                        act.wait_ge(pe_pv, nth(i, NP, n - 1))
                    b = 4 + 2 * (n % 2)
                    act.activation(pr[:, n % 2, :, :], ps[:, b:b + 2, P:512], ACT.Exp, scale=SELF_SCALE)\
                       .then_inc(a_p, 1)
                for g in range(2):
                    act.wait_ge(pe_pv, nth(i, NP, 4 * g + 4))
                    act.activation(o_raw[:, 2 * g:2 * g + 2, :], ps[:, 2 + g, :], ACT.Copy).then_inc(a_o, 1)
                if not first:
                    relu(ps, r1_h, pe_z1, a_r1, d_r1, f, 3)
                act.wait_ge(d_on, nth(i, 1, 1))
                act.activation(o_h[:], o_c, ACT.Copy).then_inc(a_oh, 1)
                act.wait_ge(pe_x1t, nth(i, 1, 1))
                act.activation(xt_h[:], ps[:, 5, :], ACT.Copy).then_inc(a_x1t, 1)
                for u in range(4):
                    act.wait_ge(pe_q2, nth(i, 4, u + 1))
                    act.activation(q2_h[:, 2 * u:2 * u + 2, :], ps[:, 6 + u % 2, :], ACT.Copy).then_inc(a_q2, 1)
                act.wait_ge(pe_mt2, nth(i, 1, 1))
                act.activation(neg_max2[:], ps[0:H, 2, 0:S], ACT.Copy, scale=-1.0).then_inc(a_nm2, 1)
                for u in range(5):
                    if u < 4:
                        for e in range(2):
                            act.wait_ge(pe_st2, nth(i, 8, 2 * u + e + 1))
                            if u >= 2:
                                act.wait_ge(pe_pv2, nth(i, 4, u - 1))
                            act.activation(probs[0:SK, 2 * (u % 2) + e, :], ps[0:SK, 4 + 2 * (u % 2) + e, :],
                                           ACT.Exp, scale=CROSS_SCALE).then_inc(a_p2, 1)
                    if u >= 1:
                        act.wait_ge(pe_pv2, nth(i, 4, u))
                        act.activation(o2[:, 2 * u - 2:2 * u, :], ps[:, 2, :], ACT.Copy).then_inc(a_o2, 1)
                for u in range(4):
                    act.wait_ge(d_o2, nth(i, 4, u + 1))
                    act.activation(high[:, 2 * u:2 * u + 2, :], o2[:, 2 * u:2 * u + 2, :], ACT.Copy)\
                       .then_inc(a_o2h, 1)

            def transposed_x2(f):
                act.wait_ge(pe_x2t, nth(f, 1, 1))
                act.activation(x2t_h[:], ps[:, 6, :], ACT.Copy).then_inc(a_x2t, 1)

            attention(0, True, None)
            with act.Fori(1, B) as i:
                attention(i, False, i - 1)
            transposed_x2(B - 1)
            for u in range(4):
                relu(ps, r0_h, pe_z0, a_r0, d_r0, B - 1, u)
            for u in range(4):
                relu(ps, r1_h, pe_z1, a_r1, d_r1, B - 1, u)

        @block.vector
        def _(dve):
            dve.memset(k_st[:].bitcast(F32), 1.0).then_inc(const_dve, 1)
            dve.memset(v[:], 1.0).then_inc(const_dve, 1)
            dve.memset(kbd_h[:].bitcast(F32), 0.0).then_inc(const_dve, 1)
            dve.wait_ge(small_in, 16 * 11)
            dve.tensor_scalar(tmp2[:], scal[:, 0:2], 0.0, None, ALU.is_lt).then_inc(coef, 1)
            dve.wait_ge(coef, 1)
            dve.scalar_tensor_tensor(sgn[:], scal[:, 0:2], 0.0, tmp2[:], ALU.is_gt, ALU.subtract).then_inc(coef, 1)
            dve.wait_ge(coef, 2)
            dve.tensor_scalar(ffn_coef[:, 0:1], sgn[:, 0:1], 2.0, None, ALU.mult).then_inc(coef, 1)
            dve.tensor_scalar(ffn_coef[:, 1:2], sgn[:, 1:2], 2.0 * R1_SCALE, None, ALU.mult).then_inc(coef, 1)
            dve.tensor_scalar(ffn_coef[:, 2:3], sgn[:, 1:2], -R1_SCALE, None, ALU.mult).then_inc(coef, 1)
            dve.tensor_tensor(tmp2[:], scal[:, 0:2], sgn[:], ALU.mult).then_inc(coef, 1)
            dve.wait_ge(coef, 6)
            dve.scalar_tensor_tensor(ffn_coef[:, 3:4], tmp2[:, 0:1], tmp2[:, 1:2], scal[:, 2:3],
                                     ALU.mult, ALU.mult).then_inc(coef, 1)
            dve.wait_ge(coef, 7)
            dve.tensor_scalar(ffn_coef[:, 3:4], ffn_coef[:, 3:4], 4.0 / R1_SCALE, None, ALU.mult).then_inc(coef, 1)
            for n, (stage, high_part, low_part) in enumerate(split):
                dve.wait_ge(w_high, n + 1)
                for (src, dst), (_, top) in zip(column_pieces(n, stage, low_part), column_pieces(n, stage, high_part)):
                    last = dve.tensor_tensor(dst, src, top.bitcast(F32), ALU.subtract)
                last.then_inc(w_low, 1)
            dve.wait_ge(kb_in, 16 * 3)
            dve.tensor_tensor(w0[:], kb0[:, 0:KD, :], kb0[:, KD:2 * KD, :], ALU.subtract).then_inc(w_bin, 1)
            dve.tensor_scalar(w1[:], kb1, ffn_coef[:, 1:2], ffn_coef[:, 2:3], ALU.mult, ALU.add).then_inc(w_bin, 1)
            dve.tensor_scalar(w2[:], kb2, 2.0, -1.0, ALU.mult, ALU.add).then_inc(w_bin, 1)
            dve.wait_ge(w_bin, 1)
            dve.tensor_scalar(w0[:], w0[:], ffn_coef[:, 0:1], None, ALU.mult).then_inc(w_bin, 1)
            dve.wait_ge(const_pool, 14)
            dve.wait_ge(const_dve, 3)
            dve.wait_ge(coef, 8)

            def layer_norm_stats(n, y, i):
                for b in range(TB):
                    dve.bn_stats(stats[:, n, b, :], y[:, b, :]).then_inc(d_bn[n], 1)
                for b in range(TB):
                    dve.wait_ge(d_bn[n], nth(i, 2, b + 1))
                    dve.sem_inc(passed_dve, 1)
                    dve.bn_aggr(mv[:, n, b, :], stats[:, n, b, :]).then_inc(d_ag[n], 1)

            def layer_norm_apply(n, dst, y, done, i):
                dve.wait_ge(g_rs[n], nth(i, 1, 1))
                for b in range(TB):
                    dve.tensor_scalar(dst[:, b, :], y[:, b, :], mv[:, n, b, 0:1], rstd[:, n, b:b + 1],
                                      ALU.subtract, ALU.mult).then_inc(done, 1)

            def relu_low(r_h, r_l, high_done, done, f, u):
                dve.wait_ge(high_done, nth(f, 4, u + 1))
                dve.scalar_tensor_tensor(r_l[:, 2 * u:2 * u + 2, :], ps[:, u % 2, :].rearrange("p (a t) -> p a t", a=2),
                                         0.0, r_h[:, 2 * u:2 * u + 2, :], ALU.max, ALU.subtract).then_inc(done, 1)

            def self_max(i, h):
                dve.wait_ge(pe_sq, nth(i, H, h + 1))
                bank = 4 + h % 4
                for b, keys in enumerate((slice(0, P), slice(S, 2 * S))):
                    k = 2 * h + b
                    width = (b + 1) * P
                    if not (isinstance(i, int) and i == 0 and k < 4):
                        dve.wait_ge(d_mx, nth(i, 2 * H, k - 3))
                    dve.sem_inc(passed_dve, 1)
                    dve.tensor_tensor_reduce(out=junk[:, k % 4, 0:width], in0=ps[:, bank, keys],
                                             in1=causal[:, b * P:b * P + width], scale=1.0, scalar=LOWEST,
                                             op0=ALU.add, op1=ALU.max, accum_out=row_max[:, b, h:h + 1])\
                       .then_inc(d_mx, 1)

            def attention(i, first, f, first_f=False):
                dve.wait_ge(a_xt, nth(i, 1, 1))
                dve.tensor_tensor(xt_l[:].rearrange("p a b -> p (a b)"), ps[:, 2, :],
                                  xt_h[:].rearrange("p a b -> p (a b)").bitcast(F32), ALU.subtract).then_inc(d_xt, 1)
                for m in range(4):
                    dve.wait_ge(a_qk, nth(i, 4, 2 * (m // 2) + 2))
                    dve.scalar_tensor_tensor(qk_l[:, m, :], ps[:, 3 + m // 2, (m % 2) * S:(m % 2 + 1) * S],
                                             bias_qk[:, m:m + 1], qk_h[:, m, :].bitcast(F32),
                                             ALU.add, ALU.subtract).then_inc(d_qk, 1)
                dve.wait_ge(pe_v, nth(i, 1, 1))
                if not first:
                    dve.wait_ge(pe_pv, nth(f, NP, NP))
                dve.tensor_tensor(v[:, :, :, 0::2].rearrange("p b h d -> p (b h) d"),
                                  ps[:, 5, :].rearrange("p (m d) -> p m d", d=HD),
                                  bias_v[:].rearrange("p b (h d) -> p (b h) d", d=HD), ALU.add).then_inc(d_v, 1)
                if not first:
                    transposed_x2(f)
                for n in range(2):
                    for e in range(2):
                        dve.wait_ge(a_k2, nth(i, 4, 2 * n + e + 1))
                        rows = slice(64 * e, 64 * e + 64)
                        dve.tensor_tensor(k2_l[rows, 4 * n:4 * n + 4, 0:SK],
                                          ps[:, 6 + n, :].rearrange("p (m t) -> p m t", m=4)[rows, :, 0:SK],
                                          kbd_h[rows, 4 * n:4 * n + 4, e, 0:SK].bitcast(F32), ALU.subtract)\
                           .then_inc(d_k2, 1)
                dve.wait_ge(pe_v2, nth(i, 2, 2))
                dve.tensor_copy(v2[:, 512:1024], ps[0:SK, 3, :]).then_inc(d_v2, 1)
                if not first:
                    for u in range(4):
                        relu_low(r0_h, r0_l, a_r0, d_r0, f, u)
                for h in range(10):
                    self_max(i, h)
                if not first:
                    relu_low(r1_h, r1_l, a_r1, d_r1, f, 0)
                for h in range(10, H):
                    self_max(i, h)
                if not first:
                    relu_low(r1_h, r1_l, a_r1, d_r1, f, 1)
                    relu_low(r1_h, r1_l, a_r1, d_r1, f, 2)
                    relu_low(r1_h, r1_l, a_r1, d_r1, f, 3)
                dve.wait_ge(o_packed, nth(i, 64, 64))
                dve.reciprocal(s_c, s_c).then_inc(d_rc, 1)
                dve.wait_ge(d_rc, nth(i, 1, 1))
                dve.tensor_tensor(o_c, o_c, s_c, ALU.mult).then_inc(d_on, 1)
                dve.wait_ge(a_oh, nth(i, 1, 1))
                dve.tensor_tensor(o_l[:], o_c, o_h[:].bitcast(F32), ALU.subtract).then_inc(d_ol, 1)
                dve.wait_ge(pe_pj, nth(i, 1, 1))
                dve.tensor_tensor(x1[:].rearrange("p a b -> p (a b)"), ps[:, 4, :],
                                  xb[:].rearrange("p a b -> p (a b)"), ALU.add).then_inc(d_y1, 1)
                dve.wait_ge(d_y1, nth(i, 1, 1))
                layer_norm_stats(0, x1, i)
                layer_norm_apply(0, x1, x1, d_x1, i)
                dve.wait_ge(a_x1t, nth(i, 1, 1))
                dve.tensor_tensor(xt_l[:].rearrange("p a b -> p (a b)"), ps[:, 5, :],
                                  xt_h[:].rearrange("p a b -> p (a b)").bitcast(F32), ALU.subtract).then_inc(d_x1t, 1)
                for u in range(5):
                    if u < 4:
                        dve.wait_ge(a_q2, nth(i, 4, u + 1))
                        dve.tensor_tensor(q2_l[:, 2 * u:2 * u + 2, :].rearrange("p a b -> p (a b)"), ps[:, 6 + u % 2, :],
                                          q2_h[:, 2 * u:2 * u + 2, :].rearrange("p a b -> p (a b)").bitcast(F32),
                                          ALU.subtract).then_inc(d_q2, 1)
                    if u >= 1:
                        for t in (2 * u - 2, 2 * u - 1):
                            dve.wait_ge(pe_sq2, nth(i, KX, t + 1))
                            dve.tensor_reduce(row_max2[:, :, 2 * t:2 * t + 2],
                                              ps[:, 4 + t % 2, :].rearrange("p (b e k) -> p b e k", b=2, e=2)[:, :, :, 0:SK],
                                              AX_X, ALU.max).then_inc(d_mx2, 1)
                dve.wait_ge(pe_pv2, nth(i, 4, 4))
                dve.reciprocal(inv_s[:], ps[:, 3, 0:S]).then_inc(d_is, 1)
                if not first:
                    ffn_sum(f, first_f)
                dve.wait_ge(inv_spread, nth(i, 64, 64))
                for u in range(5):
                    if u < 4:
                        dve.wait_ge(a_o2, nth(i, 4, u + 1))
                        o2u = o2[:, 2 * u:2 * u + 2, :]
                        dve.tensor_tensor(o2u, o2u, inv2[:, 2 * u:2 * u + 2, :], ALU.mult).then_inc(d_o2, 1)
                    if u >= 1:
                        dve.wait_ge(a_o2h, nth(i, 4, u))
                        dve.tensor_tensor(low[:, 2 * u - 2:2 * u, :], o2[:, 2 * u - 2:2 * u, :],
                                          high[:, 2 * u - 2:2 * u, :].bitcast(F32), ALU.subtract).then_inc(d_o2l, 1)
                if not first:
                    ffn_norm(f)
                dve.wait_ge(pe_wo, nth(i, 1, 1))
                dve.tensor_tensor(x2[:].rearrange("p a b -> p (a b)"), ps[:, 4, :],
                                  x1[:].rearrange("p a b -> p (a b)"), ALU.add).then_inc(d_y2, 1)
                dve.wait_ge(d_y2, nth(i, 1, 1))
                layer_norm_stats(1, x2, i)
                layer_norm_apply(1, x2, x2, d_x2, i)

            def transposed_x2(f):
                dve.wait_ge(a_x2t, nth(f, 1, 1))
                dve.tensor_tensor(x2t_l[:].rearrange("p a b -> p (a b)"), ps[:, 6, :],
                                  x2t_h[:].rearrange("p a b -> p (a b)"), ALU.subtract).then_inc(d_x2t, 1)

            def ffn_sum(f, first_f):
                if not first_f:
                    dve.wait_ge(stored, nth(f, 16, 0))
                for b in range(TB):
                    dve.wait_ge(pe_z2, nth(f, 2, b + 1))
                    dve.scalar_tensor_tensor(y3[:, b, :], ps[:, b, 0:D], ffn_coef[:, 3:4], x2[:, b, :],
                                             ALU.mult, ALU.add).then_inc(d_y3, 1)
                dve.wait_ge(d_y3, nth(f, 2, 2))
                layer_norm_stats(2, y3, f)

            def ffn_norm(f):
                layer_norm_apply(2, y3, y3, d_out, f)

            attention(0, True, None)
            attention(1, False, 0, first_f=True)
            with dve.Fori(2, B) as i:
                attention(i, False, i - 1)
            transposed_x2(B - 1)
            for u in range(4):
                relu_low(r0_h, r0_l, a_r0, d_r0, B - 1, u)
            for u in range(4):
                relu_low(r1_h, r1_l, a_r1, d_r1, B - 1, u)
            ffn_sum(B - 1, False)
            ffn_norm(B - 1)

        @block.tensor
        def _(pe):
            pe.wait_ge(const_pool, 14)
            pe.wait_ge(const_dve, 3)
            pe.wait_ge(w_low, 4)
            pe.wait_ge(wkv_in, 32)
            pe.wait_ge(w_bin, 4)

            def transposes(src, bank, i, done):
                for kk in range(KD):
                    for b in range(TB):
                        last = pe.transpose(ps[:, bank, kk * S + b * P:kk * S + (b + 1) * P],
                                            src[:, b, kk * P:(kk + 1) * P], ident[:])
                last.then_inc(done, 1)

            def weights_by_tokens(dst, w_h, w_l, cols, a_h, a_l):
                for kk in range(KD):
                    for n, (w, a) in enumerate(((w_h, a_h), (w_h, a_l), (w_l, a_h))):
                        last = pe.matmul(dst, w[:, kk, cols], a[:, kk, :], start=kk == 0 and n == 0,
                                         stop=kk == KD - 1 and n == 2)
                return last

            def tokens_by_weights(dst, a_h, a_l, b, w_h, w_l, cols, blocks):
                rows = slice(b * P, (b + 1) * P)
                for kk in range(blocks):
                    for n, (a, w) in enumerate(((a_h, w_h), (a_l, w_h), (a_h, w_l))):
                        last = pe.matmul(dst, a[:, kk, rows], w[:, kk, cols], start=kk == 0 and n == 0,
                                         stop=kk == blocks - 1 and n == 2)
                return last

            def hidden(f, w, blocks, a_h, a_l, m):
                for kk in range(blocks):
                    pe.matmul(ps[:, (m // 2) % 2, (m % 2) * S:(m % 2 + 1) * S], w[:, kk, m * P:(m + 1) * P],
                              a_h[:, kk, :], start=kk == 0, stop=False)
                    last = pe.matmul(ps[:, (m // 2) % 2, (m % 2) * S:(m % 2 + 1) * S], w[:, kk, m * P:(m + 1) * P],
                                     a_l[:, kk, :], start=False, stop=kk == blocks - 1)
                return last

            def layer0(f, u, first_f):
                if u == 0:
                    pe.wait_ge(a_x2t, nth(f, 1, 1))
                    pe.wait_ge(d_x2t, nth(f, 1, 1))
                if u < 2:
                    if not first_f:
                        pe.wait_ge(d_y3, nth(f, 2, u - 1))
                else:
                    pe.wait_ge(d_r0, nth(f, 4, u - 1))
                hidden(f, w0, KD, x2t_h, x2t_l, 2 * u)
                hidden(f, w0, KD, x2t_h, x2t_l, 2 * u + 1).then_inc(pe_z0, 1)

            def layer1(f, m):
                u = m // 2
                if m == 0:
                    pe.wait_ge(d_r0, nth(f, 4, 4))
                if m % 2 == 0 and u >= 2:
                    pe.wait_ge(d_r1, nth(f, 4, u - 1))
                last = hidden(f, w1, KF, r0_h, r0_l, m)
                if m % 2:
                    last.then_inc(pe_z1, 1)

            def layer2(f, b):
                if b == 0:
                    pe.wait_ge(d_r1, nth(f, 4, 4))
                rows = slice(b * P, (b + 1) * P)
                for kk in range(KF):
                    pe.matmul(ps[:, b, 0:D], r1_h[:, kk, rows], w2[:, kk, :], start=kk == 0, stop=False)
                    last = pe.matmul(ps[:, b, 0:D], r1_l[:, kk, rows], w2[:, kk, :], start=False, stop=kk == KF - 1)
                last.then_inc(pe_z2, 1)

            def transposed_x2(f):
                pe.wait_ge(d_x2, nth(f, 2, 2))
                transposes(x2, 6, f, pe_x2t)

            def scores_by_query(i, h):
                if h >= 4:
                    pe.wait_ge(d_mx, nth(i, 2 * H, 2 * (h - 3)))
                rows = slice(64 * (h % 2), 64 * (h % 2) + ROW_M)
                for b in range(TB):
                    last = pe.matmul(ps[:, 4 + h % 4, b * S:(b + 1) * S], q_st[rows, h // 2, b * P:(b + 1) * P],
                                     k_st[rows, h // 2, :], start=True, stop=True)
                last.then_inc(pe_sq, 1)

            def scores_by_key(i, n):
                if n >= 2:
                    pe.wait_ge(a_p, nth(i, NP, n - 1))
                for e in range(2):
                    rows = slice(64 * e, 64 * e + KST)
                    for kb in (1, 0):
                        last = pe.matmul(ps[:, 4 + 2 * (n % 2) + e, (1 - kb) * S:(2 - kb) * S],
                                         k_st[rows, n, kb * P:(kb + 1) * P], q_st[rows, n, :], start=True, stop=True)
                last.then_inc(pe_st, 1)

            def values(i, n):
                pe.wait_ge(g_p, nth(i, NP, n + 1))
                for e in range(2):
                    h = 2 * n + e
                    g, j = h // 4, h % 4
                    c = (g % 2) * S
                    rows = slice(32 * j, 32 * j + 32)
                    pe.matmul(ps[rows, 2 + g // 2, c:c + S], v[:, 0, h, :], pr[:, n % 2, e, P:3 * P],
                              start=True, stop=False)
                    last = pe.matmul(ps[rows, 2 + g // 2, c + P:c + S], v[:, 1, h, :], pr[:, n % 2, e, 0:P],
                                     start=False, stop=True)
                last.then_inc(pe_pv, 1)

            def cross_scores_by_query(i, t):
                if t >= 2:
                    pe.wait_ge(d_mx2, nth(i, KX, t - 1))
                for b in range(TB):
                    last = pe.matmul(ps[:, 4 + t % 2, b * S:(b + 1) * S], q2_h[:, t, b * P:(b + 1) * P],
                                     kbd_h[:, t, :, :].rearrange("p e k -> p (e k)"), start=True, stop=True)
                last.then_inc(pe_sq2, 1)

            def cross_scores_by_key(i, u):
                if u >= 2:
                    pe.wait_ge(a_p2, nth(i, 8, 2 * u - 2))
                for e in range(2):
                    rows = slice(64 * e, 64 * e + 64)
                    for t in (2 * u, 2 * u + 1):
                        dst = ps[0:SK, 4 + 2 * (u % 2) + e, (t % 2) * S:(t % 2 + 1) * S]
                        pe.matmul(dst, kbd_h[rows, t, e, 0:SK], q2_h[rows, t, :], start=True, stop=False)
                        pe.matmul(dst, kbd_h[rows, t, e, 0:SK], q2_l[rows, t, :], start=False, stop=False)
                        pe.matmul(dst, k2_l[rows, t, 0:SK], q2_h[rows, t, :], start=False, stop=False)
                        last = pe.matmul(dst, head_row[:, 2 * t + e, 0:SK], neg_max2[:], start=False, stop=True)
                    last.then_inc(pe_st2, 1)

            def cross_values(i, u):
                pe.wait_ge(a_p2, nth(i, 8, 2 * u + 2))
                if u >= 1:
                    pe.wait_ge(a_o2, nth(i, 4, u))
                for t in (2 * u, 2 * u + 1):
                    for e in range(2):
                        p = probs[0:SK, 2 * (u % 2) + e, (t % 2) * S:(t % 2 + 1) * S]
                        pe.matmul(ps[64 * e:64 * e + 64, 2, (t % 2) * S:(t % 2 + 1) * S],
                                  v2[:, (2 * t + e) * XD:(2 * t + e + 1) * XD], p, start=True, stop=True)
                for t in (2 * u, 2 * u + 1):
                    for e in range(2):
                        p = probs[0:SK, 2 * (u % 2) + e, (t % 2) * S:(t % 2 + 1) * S]
                        j = (2 * t + e) % 4
                        last = pe.matmul(ps[32 * j:32 * j + 32, 3, 0:S], sum_col[:, u, :], p,
                                         start=u == 0, stop=u == 3)
                last.then_inc(pe_pv2, 1)

            def attention(i, first, f, first_f=False):
                pe.wait_ge(x_loaded, nth(i, 16, 16))
                if not first:
                    pe.wait_ge(a_o2, nth(f, 4, 4))
                transposes(x_in, 2, i, pe_xt)
                pe.wait_ge(a_xt, nth(i, 1, 1))
                pe.wait_ge(d_xt, nth(i, 1, 1))
                if not first:
                    pe.wait_ge(d_is, nth(f, 1, 1))
                for m in range(4):
                    if m == 2 and not first:
                        pe.wait_ge(d_y2, nth(f, 1, 1))
                    last = weights_by_tokens(ps[:, 3 + m // 2, (m % 2) * S:(m % 2 + 1) * S], wqkv_h, wqkv_l,
                                             slice(m * P, (m + 1) * P), xt_h, xt_l)
                    if m % 2:
                        last.then_inc(pe_qk, 1)
                for b in range(TB):
                    last = tokens_by_weights(ps[:, 5, b * D:(b + 1) * D], xt_h, xt_l, b, wqkv_h, wqkv_l,
                                             slice(2 * D, 3 * D), KD)
                last.then_inc(pe_v, 1)
                if not first:
                    transposed_x2(f)
                pe.wait_ge(c_loaded, nth(i, 16, 16))
                for kk in range(KD):
                    last = pe.transpose(ps[:, 2, kk * P:kk * P + SK], c_in[:, kk * P:(kk + 1) * P], ident[0:SK, 0:SK])
                last.then_inc(pe_ct, 1)
                pe.wait_ge(a_ct, nth(i, 1, 1))
                if not first:
                    pe.wait_ge(a_x2t, nth(f, 1, 1))
                    pe.wait_ge(d_x2t, nth(f, 1, 1))
                for m in range(KX):
                    for kk in range(KD):
                        last = pe.matmul(ps[:, 6 + m // 4, (m % 4) * P:(m % 4) * P + SK], wk[:, kk, m * P:(m + 1) * P],
                                         ct[:, kk, 0:SK], start=kk == 0, stop=kk == KD - 1)
                    if m % 4 == 3:
                        last.then_inc(pe_k2, 1)
                pe.wait_ge(d_qk, nth(i, 4, 2))
                for n in range(2):
                    for kk in range(KD):
                        last = pe.matmul(ps[0:SK, 2 + n, :], ct[:, kk, 0:SK], wv[:, kk, n * 512:(n + 1) * 512],
                                         start=kk == 0, stop=kk == KD - 1)
                    last.then_inc(pe_v2, 1)
                if not first:
                    for u in range(4):
                        layer0(f, u, first_f)
                pe.wait_ge(q_stacked, nth(i, 64, 64))
                pe.wait_ge(k_stacked, nth(i, 64, 64))
                pe.wait_ge(d_qk, nth(i, 4, 4))
                pe.wait_ge(d_v, nth(i, 1, 1))
                pe.wait_ge(d_k2, nth(i, 4, 4))
                for h in range(H):
                    scores_by_query(i, h)
                    if not first and h in (3, 6, 9, 12):
                        layer1(f, h // 3 - 1)
                pe.wait_ge(d_mx, nth(i, 2 * H, 2 * H))
                pe.wait_ge(a_v2, nth(i, 1, 1))
                for b in range(TB):
                    last = pe.transpose(ps[0:H, 2, b * P:(b + 1) * P], row_max[:, b, :], ident[:])
                last.then_inc(pe_mt, 1)
                if not first:
                    layer1(f, 4)
                    layer1(f, 5)
                pe.wait_ge(max_stacked, nth(i, 32, 32))
                pe.wait_ge(a_nm, nth(i, 1, 1))
                pe.wait_ge(d_v2, nth(i, 1, 1))
                for n in range(NP + 1):
                    if n < NP:
                        scores_by_key(i, n)
                    if n >= 1:
                        values(i, n - 1)
                if not first:
                    layer1(f, 6)
                    layer1(f, 7)
                pe.wait_ge(a_oh, nth(i, 1, 1))
                pe.wait_ge(d_ol, nth(i, 1, 1))
                for b in range(TB):
                    last = tokens_by_weights(ps[:, 4, b * D:(b + 1) * D], o_h, o_l, b, wp_h, wp_l, slice(0, D), KD)
                last.then_inc(pe_pj, 1)
                if not first:
                    layer2(f, 0)
                pe.wait_ge(d_x1, nth(i, 2, 2))
                transposes(x1, 5, i, pe_x1t)
                pe.wait_ge(a_x1t, nth(i, 1, 1))
                pe.wait_ge(d_x1t, nth(i, 1, 1))
                for u in range(5):
                    if u < 4:
                        if u >= 2:
                            pe.wait_ge(d_q2, nth(i, 4, u - 1))
                        for t in (2 * u, 2 * u + 1):
                            last = weights_by_tokens(ps[:, 6 + u % 2, (t % 2) * S:(t % 2 + 1) * S], wq_h, wq_l,
                                                     slice(t * P, (t + 1) * P), xt_h, xt_l)
                        last.then_inc(pe_q2, 1)
                    if u >= 1:
                        pe.wait_ge(a_q2, nth(i, 4, u))
                        cross_scores_by_query(i, 2 * u - 2)
                        cross_scores_by_query(i, 2 * u - 1)
                pe.wait_ge(d_mx2, nth(i, KX, KX))
                for b in range(TB):
                    last = pe.transpose(ps[0:H, 2, b * P:(b + 1) * P], row_max2[:, b, :], ident[:])
                last.then_inc(pe_mt2, 1)
                pe.wait_ge(a_nm2, nth(i, 1, 1))
                pe.wait_ge(d_q2, nth(i, 4, 4))
                for u in range(5):
                    if u < 4:
                        cross_scores_by_key(i, u)
                    if u >= 1:
                        cross_values(i, u - 1)
                if not first:
                    layer2(f, 1)
                for b in range(TB):
                    rows = slice(b * P, (b + 1) * P)
                    for t in range(KX):
                        if b == 0 and t % 2 == 0:
                            pe.wait_ge(a_o2h, nth(i, 4, t // 2 + 1))
                            pe.wait_ge(d_o2l, nth(i, 4, t // 2 + 1))
                        for n, (a, w) in enumerate(((high, wo_h), (low, wo_h), (high, wo_l))):
                            last = pe.matmul(ps[:, 4, b * D:(b + 1) * D], a[:, t, rows], w[:, t, :],
                                             start=t == 0 and n == 0, stop=t == KX - 1 and n == 2)
                last.then_inc(pe_wo, 1)

            attention(0, True, None)
            attention(1, False, 0, first_f=True)
            with pe.Fori(2, B) as i:
                attention(i, False, i - 1)
            transposed_x2(B - 1)
            for u in range(4):
                layer0(B - 1, u, False)
            for m in range(KF):
                layer1(B - 1, m)
            for b in range(TB):
                layer2(B - 1, b)


_INS = ["x", "ctx_1024", "L0_attn_w_qkv", "L0_attn_b_qkv", "L0_attn_w_proj", "L0_attn_b_proj", "L0_xattn_w_q",
        "L0_xattn_w_k", "L0_xattn_w_v", "L0_xattn_w_o", "L0_ffn_k0", "L0_ffn_k1", "L0_ffn_k2", "L0_ffn_s0",
        "L0_ffn_s1", "L0_ffn_s2"]


def kernel(**inputs):
    import numpy as _np
    import concourse.bacc as _bacc
    from concourse import mybir as _mybir
    from concourse.bass_utils import run_bass_kernel_spmd as _run

    nc = _bacc.Bacc("TRN2", target_bir_lowering=False, num_devices=1)
    arrays, args = {}, []
    for name in _INS:
        a = _np.ascontiguousarray(inputs[name])
        arrays[f"in_{name}"] = a
        args.append(nc.dram_tensor(f"in_{name}", a.shape, _mybir.dt.from_np(a.dtype), kind="ExternalInput").ap())
    shape = tuple(inputs["x"].shape)
    args.append(nc.dram_tensor("out_0", shape, _mybir.dt.float32, kind="ExternalOutput").ap())
    decoder_layer(nc, *args)
    r = _run(nc, [arrays], core_ids=[0])
    return r.results[0]["out_0"]
```

```python
from contextlib import ExitStack

import concourse.bass as bass
from concourse import mybir

F32 = mybir.dt.float32
F32R = mybir.dt.float32r
F16 = mybir.dt.float16
BF16 = mybir.dt.bfloat16
U8 = mybir.dt.uint8
ALU = mybir.AluOpType
ACT = mybir.ActivationFunctionType
AX_X = mybir.AxisListType.X

P = 128
MASKED = -1e30
LOWEST = -3e38
EPS = 1e-5


def nth(i, per, k):
    return i * per + k


def decoder_layer(nc, x, ctx, w_qkv, b_qkv, w_proj, b_proj, w_q, w_k, w_v, w_o, k0, k1, k2, s0, s1, s2, out):
    B, S, D = x.shape
    SK = ctx.shape[1]
    H = 16
    HD = D // H
    XD = w_q.shape[1] // H
    F = k1.shape[0]
    KD = D // P
    TB = S // P
    NP = H // 2
    KX = w_q.shape[1] // P
    KF = F // P
    R1_SCALE = 1.0 / 16
    SELF_SCALE = float(HD) ** -0.5
    CROSS_SCALE = float(XD) ** -0.5
    ROW_M = 3 * HD
    KST = ROW_M + 1
    NQ = D // HD // 2

    with ExitStack() as stack:
        def sb(name, shape, dt):
            return stack.enter_context(nc.sbuf_tensor(name, shape, dt))

        def sem(name):
            return stack.enter_context(nc.semaphore(name))

        wqkv_h = sb("wqkv_h", [P, KD, 3 * D], F32R)
        wqkv_l = sb("wqkv_l", [P, KD, 3 * D], F32R)
        wp_h = sb("wp_h", [P, KD, D], F32R)
        wp_l = sb("wp_l", [P, KD, D], F32R)
        wq_h = sb("wq_h", [P, KD, H * XD], F32R)
        wq_l = sb("wq_l", [P, KD, H * XD], F32R)
        wk = sb("wk", [P, KD, H * XD], F32)
        wv = sb("wv", [P, KD, H * XD], F32)
        wo_h = sb("wo_h", [P, KX, D], F32R)
        wo_l = sb("wo_l", [P, KX, D], F32R)
        w0 = sb("w0", [P, KD, F], F16)
        w1 = sb("w1", [P, KF, F], F16)
        w2 = sb("w2", [P, KF, D], F16)
        bias_qk = sb("bias_qk", [P, 2 * KD], F32)
        bias_v = sb("bias_v", [P, TB, D], F32)
        bias_p = sb("bias_p", [P, TB, D], F32)
        ident = sb("ident", [P, P], F32)
        causal = sb("causal", [P, 3 * P], BF16)
        head_row = sb("head_row", [P, 4, 4, SK + 1], F32R)
        sum_col = sb("sum_col", [SK, 4, 32], F32)
        minus_half = sb("minus_half", [P, TB], F32)
        scal = sb("scal", [P, 3], F32)
        sgn = sb("sgn", [P, 2], F32)
        tmp2 = sb("tmp2", [P, 2], F32)
        ffn_coef = sb("ffn_coef", [P, 4], F32)
        x_in = sb("x_in", [P, TB, D], F32)
        xb = sb("xb", [P, TB, D], F32)
        xt_h = sb("xt_h", [P, KD, S], F32R)
        xt_l = sb("xt_l", [P, KD, S], F32R)
        low = sb("low", [P, KX, S], F32R)
        q2_l = low
        high = sb("high", [P, KX, S], F32R)
        q2_h = high
        q_st = sb("q_st", [P, NP, S], F32R)
        k_st = sb("k_st", [P, NP, S], F32R)
        v = sb("v", [P, TB, H, 2 * HD], F32)
        probs = sb("probs", [P, 4, 512], F32)
        probs_flat = probs[:].rearrange("p a b -> p (a b)")
        pr = probs_flat[:, 0:2 * 768].rearrange("p (n a b) -> p n a b", n=2, a=2)
        qk_h = probs_flat[:, 0:4 * S].bitcast(F32R).rearrange("p (m t) -> p m t", m=4)
        qk_l = probs_flat[:, 4 * S:8 * S].bitcast(F32R).rearrange("p (m t) -> p m t", m=4)
        o_h = sb("o_h", [P, KD, S], F32R)
        o_l = sb("o_l", [P, KD, S], F32R)
        x1 = sb("x1", [P, TB, D], F32)
        c_in = sb("c_in", [SK, D], F32)
        ct = sb("ct", [P, KD, SK + 1], F32)
        kbd_h = sb("kbd_h", [P, KX, 2, P], F32R)
        k2_l = sb("k2_l", [P, KX, SK + 1], F32R)
        v2 = sb("v2", [SK, H * XD], F32)
        o2 = sb("o2", [P, KX, S], F32)
        o_raw = o2[:, 0:4, :]
        o_c = o2[:, 4:6, :]
        s_c = o2[:, 6:8, :]
        inv_l = sb("inv_l", [P, S], F32R)
        x2 = sb("x2", [P, TB, D], F32)
        x2t_h = sb("x2t_h", [P, KD, S], F16)
        x2t_l = sb("x2t_l", [P, KD, S], F16)
        r0_h = sb("r0_h", [P, KF, S], F16)
        r0_l = sb("r0_l", [P, KF, S], F16)
        r1_h = sb("r1_h", [P, KF, S], F16)
        r1_l = sb("r1_l", [P, KF, S], F16)
        y3 = sb("y3", [P, TB, D], F32)
        junk = sb("junk", [P, 2, 3 * P], BF16)
        row_max = sb("row_max", [P, TB, H], F32)
        row_max2 = sb("row_max2", [P, TB, P], F32)
        inv_s = row_max2[:].rearrange("p b h -> p (b h)")
        head_rows = sb("head_rows", [P, S], F32R)
        neg_max = head_rows[0:H, :]
        neg_max2 = head_rows
        inv_h = head_rows
        stats = sb("stats", [P, 3, TB, 6], F32)
        mv = sb("mv", [P, 3, TB, 2], F32)
        var_eps = sb("var_eps", [P, 3, TB], F32)
        rstd = sb("rstd", [P, 3, TB], F32)

        ps = stack.enter_context(nc.psum_tensor("ps", [P, 8, 512], F32))

        w_in = [sem(f"w_in{n}") for n in range(4)]
        wkv_in = sem("wkv_in")
        kb_in = sem("kb_in")
        small_in = sem("small_in")
        x_loaded = sem("x_loaded")
        c_loaded = sem("c_loaded")
        q_stacked = sem("q_stacked")
        k_stacked = sem("k_stacked")
        max_stacked = sem("max_stacked")
        o_packed = sem("o_packed")
        stored = sem("stored")
        const_pool = sem("const_pool")
        const_dve = sem("const_dve")
        w_high = sem("w_high")
        w_low = sem("w_low")
        w_bin = sem("w_bin")
        coef = sem("coef")
        pe_xt, pe_qk, pe_v, pe_x2t, pe_ct, pe_k2, pe_v2 = (sem("pe_" + n) for n in "xt qk v x2t ct k2 v2".split())
        pe_sq, pe_mt, pe_st, pe_pv, pe_pj, pe_x1t = (sem("pe_" + n) for n in "sq mt st pv pj x1t".split())
        pe_q2, pe_sq2, pe_mt2, pe_st2, pe_pv2, pe_iv, pe_wo = (
            sem("pe_" + n) for n in "q2 sq2 mt2 st2 pv2 iv wo".split())
        pe_z0, pe_z1, pe_z2 = (sem("pe_" + n) for n in "z0 z1 z2".split())
        a_xt, a_qk, a_x2t, a_ct, a_k2, a_v2, a_nm, a_p, a_o, a_oh, a_x1t, a_q2, a_nm2, a_p2, a_o2, a_ih, a_o2h, a_r0, a_r1 = (
            sem("a_" + n) for n in "xt qk x2t ct k2 v2 nm p o oh x1t q2 nm2 p2 o2 ih o2h r0 r1".split())
        d_xt, d_qk, d_v, d_x2t, d_k2, d_v2, d_mx, d_rc, d_on, d_ol, d_y1, d_x1, d_x1t, d_q2, d_mx2, d_is, d_il = (
            sem("d_" + n) for n in "xt qk v x2t k2 v2 mx rc on ol y1 x1 x1t q2 mx2 is il".split())
        d_o2, d_o2l, d_y2, d_x2, d_r0, d_r1, d_y3, d_out = (
            sem("d_" + n) for n in "o2 o2l y2 x2 r0 r1 y3 out".split())
        d_bn = [sem(f"d_bn{n}") for n in range(3)]
        d_ag = [sem(f"d_ag{n}") for n in range(3)]
        g_xb, g_p = sem("g_xb"), sem("g_p")
        passed_dve, passed_pool = sem("passed_dve"), sem("passed_pool")
        g_ve = [sem(f"g_ve{n}") for n in range(3)]
        g_rs = [sem(f"g_rs{n}") for n in range(3)]

        x_rows = x.rearrange("b s d -> (b s) d")
        ctx_rows = ctx.rearrange("b s d -> (b s) d")
        out_rows = out.rearrange("b s d -> (b s) d")

        def column_pieces(n, stage, dst):
            if n:
                return [(stage, dst[:])]
            pieces = [(stage[:, :, 2 * D:], dst[:, :, 2 * D:])]
            for kk in range(KD):
                for m in range(2 * KD):
                    src = stage[:, kk, (m // 2) * D:(m // 2 + 1) * D].rearrange("p (n e d) -> p e d n", e=2, d=HD)
                    pieces.append((src[:, m % 2], dst[:, kk, m * P:(m + 1) * P].rearrange("p (d n) -> p d n", n=NP)))
            return pieces

        qk_d = nc.dram_tensor("qk_scratch", [2, P, 2 * KD, S], F32, kind="Internal").ap()
        o_d = nc.dram_tensor("o_scratch", [KD, 2, P, S], F32, kind="Internal").ap()
        qk_saved, o_saved = sem("qk_saved"), sem("o_saved")

        block = stack.enter_context(nc.Block())

        kb0 = r0_h[:].rearrange("p a b -> p (a b)").bitcast(U8).rearrange("p (k n) -> p k n", k=2 * KD)
        kb2 = r0_l[:].rearrange("p a b -> p (a b)").bitcast(U8)[:, 0:KF * D].rearrange("p (k n) -> p k n", k=KF)
        kb1 = probs[:].rearrange("p a b -> p (a b)").bitcast(U8).rearrange("p (k n) -> p k n", k=KF)
        o2_flat = o2[:].rearrange("p a b -> p (a b)")
        stage_qkv = o2_flat[:, 0:KD * 3 * D].rearrange("p (k n) -> p k n", k=KD)
        stage_p = o2_flat[:, KD * 3 * D:].rearrange("p (k n) -> p k n", k=KD)
        stage_q = o2_flat.rearrange("p (k n) -> p k n", k=KD)
        stage_o = probs_flat.rearrange("p (k n) -> p k n", k=KX)
        split = ((stage_qkv, wqkv_h, wqkv_l), (stage_p, wp_h, wp_l), (stage_q, wq_h, wq_l), (stage_o, wo_h, wo_l))

        @block.sync
        def _(sp):
            sp.dma_start(x_in[:], x[0].rearrange("(b p) d -> p b d", p=P)).then_inc(x_loaded, 16)
            sp.dma_start(c_in[:], ctx[0]).then_inc(c_loaded, 16)
            sp.dma_start(stage_qkv, w_qkv.rearrange("(k p) n -> p k n", p=P)).then_inc(w_in[0], 16)
            sp.dma_start(stage_p, w_proj.rearrange("(k p) n -> p k n", p=P)).then_inc(w_in[1], 16)
            for m in range(2 * KD):
                src = b_qkv[(m // 2) * D:(m // 2 + 1) * D].rearrange("(p e d) -> e d p", e=2, d=HD)[m % 2]
                sp.dma_start(bias_qk[:, m:m + 1], src, allow_slow_non_contiguous=True).then_inc(small_in, 16)
            for b in range(TB):
                sp.dma_start(bias_v[:, b, :], b_qkv[2 * D:3 * D].partition_broadcast(P)).then_inc(small_in, 16)
                sp.dma_start(bias_p[:, b, :], b_proj.partition_broadcast(P)).then_inc(small_in, 16)
            for n, s in enumerate((s0, s1, s2)):
                sp.dma_start(scal[:, n:n + 1], s.partition_broadcast(P)).then_inc(small_in, 16)
            sp.dma_start(kb0, k0.rearrange("(k p) n -> p k n", p=P)).then_inc(kb_in, 16)
            sp.dma_start(kb2, k2.rearrange("(k p) n -> p k n", p=P)).then_inc(kb_in, 16)
            sp.dma_start(kb1, k1.rearrange("(k p) n -> p k n", p=P)).then_inc(kb_in, 16)
            sp.dma_start(wk[:], w_k.rearrange("(k p) n -> p k n", p=P)).then_inc(wkv_in, 16)
            sp.dma_start(wv[:], w_v.rearrange("(k p) n -> p k n", p=P)).then_inc(wkv_in, 16)
            sp.wait_ge(w_low, 2)
            sp.dma_start(stage_q, w_q.rearrange("(k p) n -> p k n", p=P)).then_inc(w_in[2], 16)
            sp.wait_ge(w_bin, 2)
            sp.dma_start(stage_o, w_o.rearrange("(k p) n -> p k n", p=P)).then_inc(w_in[3], 16)
            sp.wait_ge(w_low, 4)

            def load(j):
                sp.wait_ge(pe_xt, nth(j, 1, 0))
                sp.wait_ge(g_xb, nth(j, 1, 0))
                sp.wait_ge(pe_ct, nth(j, 1, 0))
                sp.dma_start(x_in[:], x_rows[bass.ds(j * S, S), :].rearrange("(b p) d -> p b d", p=P))\
                  .then_inc(x_loaded, 16)
                sp.dma_start(c_in[:], ctx_rows[bass.ds(j * SK, SK), :]).then_inc(c_loaded, 16)

            def head_stacks(j):
                sp.wait_ge(a_qk, nth(j, 4, 4))
                sp.dma_start(qk_d[0], qk_h.bitcast(F32)).then_inc(qk_saved, 16)
                sp.wait_ge(d_qk, nth(j, 4, 4))
                sp.dma_start(qk_d[1], qk_l.bitcast(F32)).then_inc(qk_saved, 16)
                sp.wait_ge(qk_saved, nth(j, 32, 32))
                for dst, at, both, one, done in ((q_st, 0, HD, 0, q_stacked), (k_st, KD, 0, 2 * HD, k_stacked)):
                    for e in range(2):
                        src = qk_d[:, :, at + e, :].rearrange("a (d p) t -> (a d) p t", p=NP)
                        r = 64 * e + both
                        sp.dma_start(dst[r:r + 2 * HD, :, :].bitcast(F32), src).then_inc(done, 16)
                        r = 64 * e + one
                        sp.dma_start(dst[r:r + HD, :, :].bitcast(F32), src[0:HD]).then_inc(done, 16)

            def attention(i, first, f, more=True):
                if more:
                    load(i + 1)
                sp.wait_ge(a_nm, nth(i, 1, 1))
                sp.wait_ge(q_stacked, nth(i, 64, 64))
                for e in range(2):
                    sp.dma_start(q_st[64 * e + ROW_M:64 * e + ROW_M + 1, :, :].bitcast(F32),
                                 neg_max[e::2, :].bitcast(F32)).then_inc(max_stacked, 16)
                for m in range(KD):
                    sp.wait_ge(a_o, nth(i, 2, m + 1))
                    sp.dma_start(o_d[m].rearrange("e p t -> p e t"), o_raw[:, 2 * m:2 * m + 2, :]).then_inc(o_saved, 16)
                    sp.wait_ge(o_saved, nth(i, 32, 16 * m + 16))
                    rows = o_d[m].rearrange("e (r two) t -> two (e r) t", two=2)
                    for part, dst in ((1, s_c), (0, o_c)):
                        sp.dma_start(dst[:, m, :], rows[part]).then_inc(o_packed, 16)
                if not first:
                    store(f)
                if more:
                    head_stacks(i + 1)

            def store(f):
                sp.wait_ge(d_out, nth(f, 2, 2))
                sp.dma_start(out_rows[bass.ds(f * S, S), :].rearrange("(b p) d -> p b d", p=P), y3[:])\
                  .then_inc(stored, 16)

            head_stacks(0)
            attention(0, True, None)
            with sp.Fori(1, B - 1) as i:
                attention(i, False, i - 1)
            attention(B - 1, False, B - 2, more=False)
            store(B - 1)
            sp.wait_ge(stored, 16 * B)

        @block.gpsimd
        def _(pool):
            pool.memset(ident[:], 0.0).then_inc(const_pool, 1)
            pool.memset(causal[:], 0.0).then_inc(const_pool, 1)
            pool.memset(head_row[:].bitcast(F32), 1.0).then_inc(const_pool, 1)
            pool.wait_ge(const_pool, 3)
            pool.affine_select(out=ident[:], in_=ident[:], compare_op=ALU.not_equal, fill=1.0, base=0,
                               pattern=[[-1, P]], channel_multiplier=1).then_inc(const_pool, 1)
            for c in (0, 2):
                tri = causal[:, c * P:(c + 1) * P]
                pool.affine_select(out=tri, in_=tri, compare_op=ALU.is_ge, fill=MASKED, base=0,
                                   pattern=[[-1, P]], channel_multiplier=1).then_inc(const_pool, 1)
            pool.affine_select(out=head_row[:], in_=head_row[:], compare_op=ALU.is_equal, fill=0.0, base=0,
                               pattern=[[-1, 4], [-32, 4], [0, SK + 1]], channel_multiplier=1).then_inc(const_pool, 1)
            pool.memset(minus_half[:], -0.5).then_inc(const_pool, 1)
            pool.memset(sum_col[:], 0.0).then_inc(const_pool, 1)
            pool.wait_ge(const_pool, 9)
            for g in range(4):
                pool.memset(sum_col[:, g, g:g + 1], 1.0).then_inc(const_pool, 1)
            pool.memset(sum_col[:, 0, 4:32], 1.0).then_inc(const_pool, 1)
            pool.wait_ge(const_pool, 14)
            pool.wait_ge(small_in, 16 * 11)

            def biased(j):
                pool.wait_ge(x_loaded, nth(j, 16, 16))
                pool.tensor_tensor(xb[:], x_in[:], bias_p[:], ALU.add).then_inc(g_xb, 1)

            def attention(i, first, f, more=True):
                for n in range(NP):
                    pool.wait_ge(a_p, nth(i, NP, n + 1))
                    pool.sem_inc(passed_pool, 1)
                    diag = pr[:, n % 2, :, 0:2 * P].rearrange("p a (b q) -> p a b q", b=2)
                    pool.affine_select(out=diag, in_=diag, compare_op=ALU.is_ge, fill=0.0, base=0,
                                       pattern=[[0, 2], [0, 2], [1, P]], channel_multiplier=-1).then_inc(g_p, 1)
                inverse_deviation(0, i)
                if more:
                    biased(i + 1)
                if not first:
                    inverse_deviation(2, f)
                inverse_deviation(1, i)

            def inverse_deviation(n, i):
                pool.wait_ge(d_ag[n], nth(i, 2, 2))
                pool.sem_inc(passed_pool, 1)
                pool.tensor_scalar(var_eps[:, n, :], mv[:, n, :, 1], EPS, None, ALU.add).then_inc(g_ve[n], 1)
                pool.wait_ge(g_ve[n], nth(i, 1, 1))
                pool.tensor_tensor(rstd[:, n, :], var_eps[:, n, :], minus_half[:], ALU.pow).then_inc(g_rs[n], 1)

            biased(0)
            attention(0, True, None)
            with pool.Fori(1, B - 1) as i:
                attention(i, False, i - 1)
            attention(B - 1, False, B - 2, more=False)
            inverse_deviation(2, B - 1)

        @block.scalar
        def _(act):
            for n, (stage, high_part, _) in enumerate(split):
                act.wait_ge(w_in[n], 16)
                pieces = column_pieces(n, stage, high_part)
                for src, dst in pieces:
                    last = act.activation(dst, src, ACT.Copy)
                last.then_inc(w_high, 1)
            act.wait_ge(small_in, 16 * 11)

            def relu(z, r_h, pe_z, done, low_done, f, u):
                act.wait_ge(pe_z, nth(f, 4, u + 1))
                act.activation(r_h[:, 2 * u:2 * u + 2, :], ps[:, u % 2, :], ACT.Relu).then_inc(done, 1)

            def transposed_x(j):
                act.wait_ge(pe_xt, nth(j, 1, 1))
                act.activation(xt_h[:], ps[:, 3, :], ACT.Copy).then_inc(a_xt, 1)

            def queries_keys(j, u):
                act.wait_ge(pe_qk, nth(j, 2, u + 1))
                for m in (2 * u, 2 * u + 1):
                    act.activation(qk_h[:, m, :], ps[:, 6 + u, (m % 2) * S:(m % 2 + 1) * S], ACT.Identity,
                                   bias=bias_qk[:, m:m + 1]).then_inc(a_qk, 1)

            def attention(i, first, f, more=True):
                act.wait_ge(pe_ct, nth(i, 1, 1))
                act.activation(ct[:, :, 0:SK], ps[:, 2, 0:2 * P].rearrange("p (k t) -> p k t", k=2)[:, :, 0:SK],
                               ACT.Copy).then_inc(a_ct, 1)
                for n in range(2):
                    act.wait_ge(pe_k2, nth(i, 2, n + 1))
                    src = ps[:, 6 + n, :].rearrange("p (m t) -> p m t", m=4)
                    for e in range(2):
                        act.activation(kbd_h[64 * e:64 * e + 64, 4 * n:4 * n + 4, e, 0:SK],
                                       src[64 * e:64 * e + 64, :, 0:SK], ACT.Copy).then_inc(a_k2, 1)
                if not first:
                    transposed_x2(f)
                    for u in range(4):
                        relu(ps, r0_h, pe_z0, a_r0, d_r0, f, u)
                    relu(ps, r1_h, pe_z1, a_r1, d_r1, f, 0)
                    relu(ps, r1_h, pe_z1, a_r1, d_r1, f, 1)
                act.wait_ge(pe_mt, nth(i, 1, 1))
                act.activation(neg_max[:], ps[0:H, 2, 0:S], ACT.Copy, scale=-1.0).then_inc(a_nm, 1)
                if not first:
                    relu(ps, r1_h, pe_z1, a_r1, d_r1, f, 2)
                for n in range(NP):
                    act.wait_ge(pe_st, nth(i, NP, n + 1))
                    if n >= 2:
                        act.wait_ge(pe_pv, nth(i, NP, n - 1))
                    b = 4 + 2 * (n % 2)
                    act.activation(pr[:, n % 2, :, :], ps[:, b:b + 2, P:512], ACT.Exp, scale=SELF_SCALE)\
                       .then_inc(a_p, 1)
                    if n in (5, NP - 1):
                        m = n // 6
                        act.wait_ge(pe_pv, nth(i, NP, 4 * m + 4))
                        act.activation(o_raw[:, 2 * m:2 * m + 2, :], ps[:, 2 + m, :], ACT.Copy).then_inc(a_o, 1)
                act.wait_ge(d_on, nth(i, 2, 1))
                act.activation(o_h[:, 0, :], o_c[:, 0, :], ACT.Copy).then_inc(a_oh, 1)
                if not first:
                    relu(ps, r1_h, pe_z1, a_r1, d_r1, f, 3)
                act.wait_ge(pe_v2, nth(i, 2, 1))
                act.activation(v2[:, 0:512], ps[0:SK, 5, :], ACT.Copy).then_inc(a_v2, 1)
                act.wait_ge(d_on, nth(i, 2, 2))
                act.activation(o_h[:, 1, :], o_c[:, 1, :], ACT.Copy).then_inc(a_oh, 1)
                act.wait_ge(pe_x1t, nth(i, 1, 1))
                act.activation(xt_h[:], ps[:, 6, :], ACT.Copy).then_inc(a_x1t, 1)
                for u in range(4):
                    act.wait_ge(pe_q2, nth(i, 4, u + 1))
                    act.activation(q2_h[:, 2 * u:2 * u + 2, :], ps[:, 6 + u % 2, :], ACT.Copy).then_inc(a_q2, 1)
                act.wait_ge(pe_mt2, nth(i, 1, 1))
                act.activation(neg_max2[:], ps[:, 2, 0:S], ACT.Copy, scale=-1.0).then_inc(a_nm2, 1)
                if more:
                    transposed_x(i + 1)
                for u in range(5):
                    if u < 4:
                        for e in range(2):
                            act.wait_ge(pe_st2, nth(i, 8, 2 * u + e + 1))
                            if u >= 2:
                                act.wait_ge(pe_pv2, nth(i, 4, u - 1))
                            act.activation(probs[0:SK, 2 * (u % 2) + e, :], ps[0:SK, 4 + 2 * (u % 2) + e, :],
                                           ACT.Exp, scale=CROSS_SCALE).then_inc(a_p2, 1)
                    if u >= 1:
                        act.wait_ge(pe_pv2, nth(i, 4, u))
                        act.activation(o2[:, 2 * u - 2:2 * u, :], ps[:, 2, :], ACT.Copy).then_inc(a_o2, 1)
                if more:
                    queries_keys(i + 1, 0)
                act.wait_ge(d_is, nth(i, 1, 1))
                act.activation(inv_h[:], inv_s, ACT.Copy).then_inc(a_ih, 1)
                if more:
                    queries_keys(i + 1, 1)
                for u in range(4):
                    act.wait_ge(d_o2, nth(i, 4, u + 1))
                    act.activation(high[:, 2 * u:2 * u + 2, :], o2[:, 2 * u:2 * u + 2, :], ACT.Copy)\
                       .then_inc(a_o2h, 1)

            def transposed_x2(f):
                act.wait_ge(pe_x2t, nth(f, 1, 1))
                act.activation(x2t_h[:], ps[:, 3, :], ACT.Copy).then_inc(a_x2t, 1)

            transposed_x(0)
            queries_keys(0, 0)
            queries_keys(0, 1)
            attention(0, True, None)
            with act.Fori(1, B - 1) as i:
                attention(i, False, i - 1)
            attention(B - 1, False, B - 2, more=False)
            transposed_x2(B - 1)
            for u in range(4):
                relu(ps, r0_h, pe_z0, a_r0, d_r0, B - 1, u)
            for u in range(4):
                relu(ps, r1_h, pe_z1, a_r1, d_r1, B - 1, u)

        @block.vector
        def _(dve):
            dve.memset(k_st[:].bitcast(F32), 1.0).then_inc(const_dve, 1)
            dve.memset(v[:], 1.0).then_inc(const_dve, 1)
            dve.memset(kbd_h[:].bitcast(F32), 0.0).then_inc(const_dve, 1)
            dve.memset(row_max2[:], 0.0).then_inc(const_dve, 1)
            dve.wait_ge(small_in, 16 * 11)
            dve.tensor_scalar(tmp2[:], scal[:, 0:2], 0.0, None, ALU.is_lt).then_inc(coef, 1)
            dve.wait_ge(coef, 1)
            dve.scalar_tensor_tensor(sgn[:], scal[:, 0:2], 0.0, tmp2[:], ALU.is_gt, ALU.subtract).then_inc(coef, 1)
            dve.wait_ge(coef, 2)
            dve.tensor_scalar(ffn_coef[:, 0:1], sgn[:, 0:1], 2.0, None, ALU.mult).then_inc(coef, 1)
            dve.tensor_scalar(ffn_coef[:, 1:2], sgn[:, 1:2], 2.0 * R1_SCALE, None, ALU.mult).then_inc(coef, 1)
            dve.tensor_scalar(ffn_coef[:, 2:3], sgn[:, 1:2], -R1_SCALE, None, ALU.mult).then_inc(coef, 1)
            dve.tensor_tensor(tmp2[:], scal[:, 0:2], sgn[:], ALU.mult).then_inc(coef, 1)
            dve.wait_ge(coef, 6)
            dve.scalar_tensor_tensor(ffn_coef[:, 3:4], tmp2[:, 0:1], tmp2[:, 1:2], scal[:, 2:3],
                                     ALU.mult, ALU.mult).then_inc(coef, 1)
            dve.wait_ge(coef, 7)
            dve.tensor_scalar(ffn_coef[:, 3:4], ffn_coef[:, 3:4], 4.0 / R1_SCALE, None, ALU.mult).then_inc(coef, 1)
            def split_low(n):
                stage, high_part, low_part = split[n]
                dve.wait_ge(w_high, n + 1)
                for (src, dst), (_, top) in zip(column_pieces(n, stage, low_part), column_pieces(n, stage, high_part)):
                    last = dve.tensor_tensor(dst, src, top.bitcast(F32), ALU.subtract)
                last.then_inc(w_low, 1)

            split_low(0)
            split_low(1)
            dve.wait_ge(kb_in, 16 * 3)
            dve.tensor_tensor(w0[:], kb0[:, 0:KD, :], kb0[:, KD:2 * KD, :], ALU.subtract).then_inc(w_bin, 1)
            dve.tensor_scalar(w1[:], kb1, ffn_coef[:, 1:2], ffn_coef[:, 2:3], ALU.mult, ALU.add).then_inc(w_bin, 1)
            dve.tensor_scalar(w2[:], kb2, 2.0, -1.0, ALU.mult, ALU.add).then_inc(w_bin, 1)
            dve.wait_ge(w_bin, 1)
            dve.tensor_scalar(w0[:], w0[:], ffn_coef[:, 0:1], None, ALU.mult).then_inc(w_bin, 1)
            split_low(2)
            split_low(3)
            dve.wait_ge(const_pool, 14)
            dve.wait_ge(const_dve, 4)
            dve.wait_ge(coef, 8)

            def layer_norm_stats(n, y, i):
                for b in range(TB):
                    dve.bn_stats(stats[:, n, b, :], y[:, b, :]).then_inc(d_bn[n], 1)
                for b in range(TB):
                    dve.wait_ge(d_bn[n], nth(i, 2, b + 1))
                    dve.sem_inc(passed_dve, 1)
                    dve.bn_aggr(mv[:, n, b, :], stats[:, n, b, :]).then_inc(d_ag[n], 1)

            def layer_norm_apply(n, dst, y, done, i):
                dve.wait_ge(g_rs[n], nth(i, 1, 1))
                for b in range(TB):
                    dve.tensor_scalar(dst[:, b, :], y[:, b, :], mv[:, n, b, 0:1], rstd[:, n, b:b + 1],
                                      ALU.subtract, ALU.mult).then_inc(done, 1)

            def relu_low(r_h, r_l, high_done, done, f, u):
                dve.wait_ge(high_done, nth(f, 4, u + 1))
                dve.scalar_tensor_tensor(r_l[:, 2 * u:2 * u + 2, :], ps[:, u % 2, :].rearrange("p (a t) -> p a t", a=2),
                                         0.0, r_h[:, 2 * u:2 * u + 2, :], ALU.max, ALU.subtract).then_inc(done, 1)

            def self_max(i, h):
                dve.wait_ge(pe_sq, nth(i, H, h + 1))
                bank = 4 + h % 4
                for b, keys in enumerate((slice(0, P), slice(S, 2 * S))):
                    k = 2 * h + b
                    width = (b + 1) * P
                    if not (isinstance(i, int) and i == 0 and k < 4):
                        dve.wait_ge(d_mx, nth(i, 2 * H, k - 3))
                    dve.sem_inc(passed_dve, 1)
                    dve.tensor_tensor_reduce(out=junk[:, h % 2, b * P:b * P + width], in0=ps[:, bank, keys],
                                             in1=causal[:, b * P:b * P + width], scale=1.0, scalar=LOWEST,
                                             op0=ALU.add, op1=ALU.max, accum_out=row_max[:, b, h:h + 1])\
                       .then_inc(d_mx, 1)

            def transposed_x(j):
                dve.wait_ge(a_xt, nth(j, 1, 1))
                dve.tensor_tensor(xt_l[:].rearrange("p a b -> p (a b)"), ps[:, 3, :],
                                  xt_h[:].rearrange("p a b -> p (a b)").bitcast(F32), ALU.subtract).then_inc(d_xt, 1)

            def queries_keys(j, m):
                dve.wait_ge(a_qk, nth(j, 4, 2 * (m // 2) + 2))
                dve.scalar_tensor_tensor(qk_l[:, m, :], ps[:, 6 + m // 2, (m % 2) * S:(m % 2 + 1) * S],
                                         bias_qk[:, m:m + 1], qk_h[:, m, :].bitcast(F32),
                                         ALU.add, ALU.subtract).then_inc(d_qk, 1)

            def self_values(j):
                dve.wait_ge(pe_v, nth(j, 1, 1))
                dve.tensor_tensor(v[:, :, :, 0::2].rearrange("p b h d -> p (b h) d"),
                                  ps[:, 5, :].rearrange("p (m d) -> p m d", d=HD),
                                  bias_v[:].rearrange("p b (h d) -> p (b h) d", d=HD), ALU.add).then_inc(d_v, 1)

            def self_output(i, m):
                dve.wait_ge(o_packed, nth(i, 64, 32 * m + 32))
                dve.reciprocal(s_c[:, m, :], s_c[:, m, :]).then_inc(d_rc, 1)
                dve.wait_ge(d_rc, nth(i, 2, m + 1))
                dve.tensor_tensor(o_c[:, m, :], o_c[:, m, :], s_c[:, m, :], ALU.mult).then_inc(d_on, 1)

            def self_output_low(i, m):
                dve.wait_ge(a_oh, nth(i, 2, m + 1))
                dve.tensor_tensor(o_l[:, m, :], o_c[:, m, :], o_h[:, m, :].bitcast(F32), ALU.subtract).then_inc(d_ol, 1)

            def attention(i, first, f, first_f=False, more=True):
                for n in range(2):
                    for e in range(2):
                        dve.wait_ge(a_k2, nth(i, 4, 2 * n + e + 1))
                        rows = slice(64 * e, 64 * e + 64)
                        dve.tensor_tensor(k2_l[rows, 4 * n:4 * n + 4, 0:SK],
                                          ps[:, 6 + n, :].rearrange("p (m t) -> p m t", m=4)[rows, :, 0:SK],
                                          kbd_h[rows, 4 * n:4 * n + 4, e, 0:SK].bitcast(F32), ALU.subtract)\
                           .then_inc(d_k2, 1)
                if not first:
                    transposed_x2(f)
                    for u in range(4):
                        relu_low(r0_h, r0_l, a_r0, d_r0, f, u)
                for h in range(10):
                    self_max(i, h)
                if not first:
                    relu_low(r1_h, r1_l, a_r1, d_r1, f, 0)
                for h in range(10, H):
                    self_max(i, h)
                if not first:
                    relu_low(r1_h, r1_l, a_r1, d_r1, f, 1)
                    relu_low(r1_h, r1_l, a_r1, d_r1, f, 2)
                self_output(i, 0)
                self_output_low(i, 0)
                if not first:
                    relu_low(r1_h, r1_l, a_r1, d_r1, f, 3)
                self_output(i, 1)
                self_output_low(i, 1)
                dve.wait_ge(pe_v2, nth(i, 2, 2))
                dve.tensor_copy(v2[:, 512:1024], ps[0:SK, 7, :]).then_inc(d_v2, 1)
                dve.wait_ge(pe_pj, nth(i, 1, 1))
                dve.tensor_tensor(x1[:].rearrange("p a b -> p (a b)"), ps[:, 4, :],
                                  xb[:].rearrange("p a b -> p (a b)"), ALU.add).then_inc(d_y1, 1)
                dve.wait_ge(d_y1, nth(i, 1, 1))
                layer_norm_stats(0, x1, i)
                layer_norm_apply(0, x1, x1, d_x1, i)
                dve.wait_ge(a_x1t, nth(i, 1, 1))
                dve.tensor_tensor(xt_l[:].rearrange("p a b -> p (a b)"), ps[:, 6, :],
                                  xt_h[:].rearrange("p a b -> p (a b)").bitcast(F32), ALU.subtract).then_inc(d_x1t, 1)
                for u in range(5):
                    if u < 4:
                        dve.wait_ge(a_q2, nth(i, 4, u + 1))
                        dve.tensor_tensor(q2_l[:, 2 * u:2 * u + 2, :].rearrange("p a b -> p (a b)"), ps[:, 6 + u % 2, :],
                                          q2_h[:, 2 * u:2 * u + 2, :].rearrange("p a b -> p (a b)").bitcast(F32),
                                          ALU.subtract).then_inc(d_q2, 1)
                    if u >= 1:
                        for t in (2 * u - 2, 2 * u - 1):
                            dve.wait_ge(pe_sq2, nth(i, KX, t + 1))
                            at = 64 * (t % 2) + t // 2
                            dve.tensor_reduce(row_max2[:, :, at:at + 33:32],
                                              ps[:, 4 + t % 2, :].rearrange("p (b e k) -> p b e k", b=2, e=2)[:, :, :, 0:SK],
                                              AX_X, ALU.max).then_inc(d_mx2, 1)
                if more:
                    transposed_x(i + 1)
                if not first:
                    ffn_sum(f, first_f)
                    ffn_norm(f)
                dve.wait_ge(pe_pv2, nth(i, 4, 4))
                dve.reciprocal(inv_s, ps[:, 3, 0:S]).then_inc(d_is, 1)
                dve.wait_ge(a_ih, nth(i, 1, 1))
                dve.tensor_tensor(inv_l[:], inv_s, inv_h[:].bitcast(F32), ALU.subtract).then_inc(d_il, 1)
                if more:
                    queries_keys(i + 1, 0)
                    queries_keys(i + 1, 1)
                for u in range(5):
                    if u < 4:
                        dve.wait_ge(pe_iv, nth(i, 4, u + 1))
                        dve.wait_ge(a_o2, nth(i, 4, u + 1))
                        o2u = o2[:, 2 * u:2 * u + 2, :].rearrange("p a b -> p (a b)")
                        dve.tensor_tensor(o2u, o2u, ps[:, 2 + u % 2, :], ALU.mult).then_inc(d_o2, 1)
                    if u < 2 and more:
                        queries_keys(i + 1, u + 2)
                    if u >= 1:
                        dve.wait_ge(a_o2h, nth(i, 4, u))
                        dve.tensor_tensor(low[:, 2 * u - 2:2 * u, :], o2[:, 2 * u - 2:2 * u, :],
                                          high[:, 2 * u - 2:2 * u, :].bitcast(F32), ALU.subtract).then_inc(d_o2l, 1)
                if more:
                    self_values(i + 1)
                dve.wait_ge(pe_wo, nth(i, 1, 1))
                dve.tensor_tensor(x2[:].rearrange("p a b -> p (a b)"), ps[:, 4, :],
                                  x1[:].rearrange("p a b -> p (a b)"), ALU.add).then_inc(d_y2, 1)
                dve.wait_ge(d_y2, nth(i, 1, 1))
                layer_norm_stats(1, x2, i)
                layer_norm_apply(1, x2, x2, d_x2, i)

            def transposed_x2(f):
                dve.wait_ge(a_x2t, nth(f, 1, 1))
                dve.tensor_tensor(x2t_l[:].rearrange("p a b -> p (a b)"), ps[:, 3, :],
                                  x2t_h[:].rearrange("p a b -> p (a b)"), ALU.subtract).then_inc(d_x2t, 1)

            def ffn_sum(f, first_f):
                if not first_f:
                    dve.wait_ge(stored, nth(f, 16, 0))
                for b in range(TB):
                    dve.wait_ge(pe_z2, nth(f, 2, b + 1))
                    dve.scalar_tensor_tensor(y3[:, b, :], ps[:, b, 0:D], ffn_coef[:, 3:4], x2[:, b, :],
                                             ALU.mult, ALU.add).then_inc(d_y3, 1)
                dve.wait_ge(d_y3, nth(f, 2, 2))
                layer_norm_stats(2, y3, f)

            def ffn_norm(f):
                layer_norm_apply(2, y3, y3, d_out, f)

            transposed_x(0)
            for m in range(4):
                queries_keys(0, m)
            self_values(0)
            attention(0, True, None)
            attention(1, False, 0, first_f=True)
            with dve.Fori(2, B - 1) as i:
                attention(i, False, i - 1)
            attention(B - 1, False, B - 2, more=False)
            transposed_x2(B - 1)
            for u in range(4):
                relu_low(r0_h, r0_l, a_r0, d_r0, B - 1, u)
            for u in range(4):
                relu_low(r1_h, r1_l, a_r1, d_r1, B - 1, u)
            ffn_sum(B - 1, False)
            ffn_norm(B - 1)

        @block.tensor
        def _(pe):
            pe.wait_ge(const_pool, 14)
            pe.wait_ge(const_dve, 4)
            pe.wait_ge(w_low, 4)
            pe.wait_ge(wkv_in, 32)
            pe.wait_ge(w_bin, 4)

            def transposes(src, bank, i, done):
                for kk in range(KD):
                    for b in range(TB):
                        last = pe.transpose(ps[:, bank, kk * S + b * P:kk * S + (b + 1) * P],
                                            src[:, b, kk * P:(kk + 1) * P], ident[:])
                last.then_inc(done, 1)

            def weights_by_tokens(dst, w_h, w_l, cols, a_h, a_l):
                for kk in range(KD):
                    for n, (w, a) in enumerate(((w_h, a_h), (w_h, a_l), (w_l, a_h))):
                        last = pe.matmul(dst, w[:, kk, cols], a[:, kk, :], start=kk == 0 and n == 0,
                                         stop=kk == KD - 1 and n == 2)
                return last

            def tokens_by_weights(dst, a_h, a_l, b, w_h, w_l, cols, blocks):
                rows = slice(b * P, (b + 1) * P)
                for kk in range(blocks):
                    for n, (a, w) in enumerate(((a_h, w_h), (a_l, w_h), (a_h, w_l))):
                        last = pe.matmul(dst, a[:, kk, rows], w[:, kk, cols], start=kk == 0 and n == 0,
                                         stop=kk == blocks - 1 and n == 2)
                return last

            def hidden(f, w, blocks, a_h, a_l, m):
                for kk in range(blocks):
                    pe.matmul(ps[:, (m // 2) % 2, (m % 2) * S:(m % 2 + 1) * S], w[:, kk, m * P:(m + 1) * P],
                              a_h[:, kk, :], start=kk == 0, stop=False)
                    last = pe.matmul(ps[:, (m // 2) % 2, (m % 2) * S:(m % 2 + 1) * S], w[:, kk, m * P:(m + 1) * P],
                                     a_l[:, kk, :], start=False, stop=kk == blocks - 1)
                return last

            def layer0(f, u, first_f):
                if u == 0:
                    pe.wait_ge(a_x2t, nth(f, 1, 1))
                    pe.wait_ge(d_x2t, nth(f, 1, 1))
                if u < 2:
                    if not first_f:
                        pe.wait_ge(d_y3, nth(f, 2, u - 1))
                else:
                    pe.wait_ge(d_r0, nth(f, 4, u - 1))
                hidden(f, w0, KD, x2t_h, x2t_l, 2 * u)
                hidden(f, w0, KD, x2t_h, x2t_l, 2 * u + 1).then_inc(pe_z0, 1)

            def layer1(f, m):
                u = m // 2
                if m == 0:
                    pe.wait_ge(d_r0, nth(f, 4, 4))
                if m % 2 == 0 and u >= 2:
                    pe.wait_ge(d_r1, nth(f, 4, u - 1))
                last = hidden(f, w1, KF, r0_h, r0_l, m)
                if m % 2:
                    last.then_inc(pe_z1, 1)

            def layer2(f, b):
                if b == 0:
                    pe.wait_ge(d_r1, nth(f, 4, 4))
                rows = slice(b * P, (b + 1) * P)
                for kk in range(KF):
                    pe.matmul(ps[:, b, 0:D], r1_h[:, kk, rows], w2[:, kk, :], start=kk == 0, stop=False)
                    last = pe.matmul(ps[:, b, 0:D], r1_l[:, kk, rows], w2[:, kk, :], start=False, stop=kk == KF - 1)
                last.then_inc(pe_z2, 1)

            def transposed_x2(f):
                pe.wait_ge(d_x2, nth(f, 2, 2))
                transposes(x2, 3, f, pe_x2t)

            def scores_by_query(i, h):
                if h >= 4:
                    pe.wait_ge(d_mx, nth(i, 2 * H, 2 * (h - 3)))
                rows = slice(64 * (h % 2), 64 * (h % 2) + ROW_M)
                for b in range(TB):
                    last = pe.matmul(ps[:, 4 + h % 4, b * S:(b + 1) * S], q_st[rows, h // 2, b * P:(b + 1) * P],
                                     k_st[rows, h // 2, :], start=True, stop=True)
                last.then_inc(pe_sq, 1)

            def scores_by_key(i, n):
                if n >= 2:
                    pe.wait_ge(a_p, nth(i, NP, n - 1))
                for e in range(2):
                    rows = slice(64 * e, 64 * e + KST)
                    for kb in (1, 0):
                        last = pe.matmul(ps[:, 4 + 2 * (n % 2) + e, (1 - kb) * S:(2 - kb) * S],
                                         k_st[rows, n, kb * P:(kb + 1) * P], q_st[rows, n, :], start=True, stop=True)
                last.then_inc(pe_st, 1)

            def values(i, n):
                pe.wait_ge(g_p, nth(i, NP, n + 1))
                for e in range(2):
                    h = 2 * n + e
                    g, j = h // 4, h % 4
                    c = (g % 2) * S
                    rows = slice(32 * j, 32 * j + 32)
                    pe.matmul(ps[rows, 2 + g // 2, c:c + S], v[:, 0, h, :], pr[:, n % 2, e, P:3 * P],
                              start=True, stop=False)
                    last = pe.matmul(ps[rows, 2 + g // 2, c + P:c + S], v[:, 1, h, :], pr[:, n % 2, e, 0:P],
                                     start=False, stop=True)
                last.then_inc(pe_pv, 1)

            def cross_scores_by_query(i, t):
                if t >= 2:
                    pe.wait_ge(d_mx2, nth(i, KX, t - 1))
                for b in range(TB):
                    last = pe.matmul(ps[:, 4 + t % 2, b * S:(b + 1) * S], q2_h[:, t, b * P:(b + 1) * P],
                                     kbd_h[:, t, :, :].rearrange("p e k -> p (e k)"), start=True, stop=True)
                last.then_inc(pe_sq2, 1)

            def cross_scores_by_key(i, u):
                if u >= 2:
                    pe.wait_ge(a_p2, nth(i, 8, 2 * u - 2))
                for e in range(2):
                    rows = slice(64 * e, 64 * e + 64)
                    for t in (2 * u, 2 * u + 1):
                        dst = ps[0:SK, 4 + 2 * (u % 2) + e, (t % 2) * S:(t % 2 + 1) * S]
                        pe.matmul(dst, kbd_h[:, t, e, 0:SK], q2_h[:, t, :], start=True, stop=False)
                        pe.matmul(dst, kbd_h[:, t, e, 0:SK], q2_l[:, t, :], start=False, stop=False)
                        pe.matmul(dst, k2_l[rows, t, 0:SK], q2_h[rows, t, :], start=False, stop=False)
                        last = pe.matmul(dst, head_row[:, t // 2, 2 * (t % 2) + e, 0:SK], neg_max2[:],
                                         start=False, stop=True)
                    last.then_inc(pe_st2, 1)

            def cross_values(i, u):
                pe.wait_ge(a_p2, nth(i, 8, 2 * u + 2))
                if u >= 1:
                    pe.wait_ge(a_o2, nth(i, 4, u))
                for t in (2 * u, 2 * u + 1):
                    for e in range(2):
                        p = probs[0:SK, 2 * (u % 2) + e, (t % 2) * S:(t % 2 + 1) * S]
                        pe.matmul(ps[64 * e:64 * e + 64, 2, (t % 2) * S:(t % 2 + 1) * S],
                                  v2[:, (2 * t + e) * XD:(2 * t + e + 1) * XD], p, start=True, stop=True)
                for t in (2 * u, 2 * u + 1):
                    for e in range(2):
                        p = probs[0:SK, 2 * (u % 2) + e, (t % 2) * S:(t % 2 + 1) * S]
                        j = (2 * t + e) % 4
                        last = pe.matmul(ps[32 * j:32 * j + 32, 3, 0:S], sum_col[:, u, :], p,
                                         start=u == 0, stop=u == 3)
                last.then_inc(pe_pv2, 1)

            def queries_keys(j):
                pe.wait_ge(a_xt, nth(j, 1, 1))
                pe.wait_ge(d_xt, nth(j, 1, 1))
                for m in range(4):
                    last = weights_by_tokens(ps[:, 6 + m // 2, (m % 2) * S:(m % 2 + 1) * S], wqkv_h, wqkv_l,
                                             slice(m * P, (m + 1) * P), xt_h, xt_l)
                    if m % 2:
                        last.then_inc(pe_qk, 1)

            def self_values(j):
                for b in range(TB):
                    last = tokens_by_weights(ps[:, 5, b * D:(b + 1) * D], xt_h, xt_l, b, wqkv_h, wqkv_l,
                                             slice(2 * D, 3 * D), KD)
                last.then_inc(pe_v, 1)

            def spread_inverse(i, u):
                if u >= 2:
                    pe.wait_ge(d_o2, nth(i, 4, u - 1))
                for t in (2 * u, 2 * u + 1):
                    dst = ps[:, 2 + u % 2, (t % 2) * S:(t % 2 + 1) * S]
                    seam = (2 * t + 1) * (SK + 1)
                    pair = head_row[:].rearrange("p u j k -> p (u j k)")[:, seam - XD:seam + XD]
                    pe.matmul(dst, pair, inv_h[:], start=True, stop=False)
                    last = pe.matmul(dst, pair, inv_l[:], start=False, stop=True)
                last.then_inc(pe_iv, 1)

            def attention(i, first, f, first_f=False, more=True):
                pe.wait_ge(c_loaded, nth(i, 16, 16))
                for kk in range(KD):
                    last = pe.transpose(ps[:, 2, kk * P:kk * P + SK], c_in[:, kk * P:(kk + 1) * P], ident[0:SK, 0:SK])
                last.then_inc(pe_ct, 1)
                pe.wait_ge(a_ct, nth(i, 1, 1))
                pe.wait_ge(d_qk, nth(i, 4, 4))
                for m in range(KX):
                    for kk in range(KD):
                        last = pe.matmul(ps[:, 6 + m // 4, (m % 4) * P:(m % 4) * P + SK], wk[:, kk, m * P:(m + 1) * P],
                                         ct[:, kk, 0:SK], start=kk == 0, stop=kk == KD - 1)
                    if m % 4 == 3:
                        last.then_inc(pe_k2, 1)
                if not first:
                    transposed_x2(f)
                    for u in range(4):
                        layer0(f, u, first_f)
                pe.wait_ge(q_stacked, nth(i, 64, 64))
                pe.wait_ge(k_stacked, nth(i, 64, 64))
                pe.wait_ge(d_v, nth(i, 1, 1))
                pe.wait_ge(d_k2, nth(i, 4, 4))
                for h in range(H):
                    scores_by_query(i, h)
                    if not first and h in (3, 6, 9, 12):
                        layer1(f, h // 3 - 1)
                pe.wait_ge(d_mx, nth(i, 2 * H, 2 * H))
                for b in range(TB):
                    last = pe.transpose(ps[0:H, 2, b * P:(b + 1) * P], row_max[:, b, :], ident[:])
                last.then_inc(pe_mt, 1)
                if not first:
                    layer1(f, 4)
                    layer1(f, 5)
                pe.wait_ge(max_stacked, nth(i, 32, 32))
                pe.wait_ge(a_nm, nth(i, 1, 1))
                for n in range(NP + 1):
                    if n < NP:
                        scores_by_key(i, n)
                    if n >= 1:
                        values(i, n - 1)
                if not first:
                    layer1(f, 6)
                    layer1(f, 7)
                for n in range(2):
                    for kk in range(KD):
                        last = pe.matmul(ps[0:SK, 5 + 2 * n, :], ct[:, kk, 0:SK], wv[:, kk, n * 512:(n + 1) * 512],
                                         start=kk == 0, stop=kk == KD - 1)
                    last.then_inc(pe_v2, 1)
                pe.wait_ge(a_oh, nth(i, 2, 2))
                pe.wait_ge(d_ol, nth(i, 2, 2))
                for b in range(TB):
                    last = tokens_by_weights(ps[:, 4, b * D:(b + 1) * D], o_h, o_l, b, wp_h, wp_l, slice(0, D), KD)
                last.then_inc(pe_pj, 1)
                if not first:
                    layer2(f, 0)
                    layer2(f, 1)
                pe.wait_ge(d_x1, nth(i, 2, 2))
                transposes(x1, 6, i, pe_x1t)
                pe.wait_ge(a_x1t, nth(i, 1, 1))
                pe.wait_ge(d_x1t, nth(i, 1, 1))
                pe.wait_ge(a_v2, nth(i, 1, 1))
                pe.wait_ge(d_v2, nth(i, 1, 1))
                for u in range(5):
                    if u < 4:
                        if u >= 2:
                            pe.wait_ge(d_q2, nth(i, 4, u - 1))
                        for t in (2 * u, 2 * u + 1):
                            last = weights_by_tokens(ps[:, 6 + u % 2, (t % 2) * S:(t % 2 + 1) * S], wq_h, wq_l,
                                                     slice(t * P, (t + 1) * P), xt_h, xt_l)
                        last.then_inc(pe_q2, 1)
                    if u >= 1:
                        pe.wait_ge(a_q2, nth(i, 4, u))
                        cross_scores_by_query(i, 2 * u - 2)
                        cross_scores_by_query(i, 2 * u - 1)
                pe.wait_ge(d_mx2, nth(i, KX, KX))
                for b in range(TB):
                    last = pe.transpose(ps[:, 2, b * P:(b + 1) * P], row_max2[:, b, :], ident[:])
                last.then_inc(pe_mt2, 1)
                if more:
                    pe.wait_ge(x_loaded, nth(i + 1, 16, 16))
                    transposes(x_in, 3, i + 1, pe_xt)
                pe.wait_ge(a_nm2, nth(i, 1, 1))
                pe.wait_ge(d_q2, nth(i, 4, 4))
                for u in range(5):
                    if u < 4:
                        cross_scores_by_key(i, u)
                    if u == 1 and more:
                        pe.wait_ge(d_xt, nth(i + 1, 1, 1))
                    if u >= 1:
                        cross_values(i, u - 1)
                if more:
                    queries_keys(i + 1)
                pe.wait_ge(a_ih, nth(i, 1, 1))
                pe.wait_ge(d_il, nth(i, 1, 1))
                pe.wait_ge(a_o2, nth(i, 4, 4))
                spread_inverse(i, 0)
                spread_inverse(i, 1)
                if more:
                    self_values(i + 1)
                spread_inverse(i, 2)
                spread_inverse(i, 3)
                for b in range(TB):
                    rows = slice(b * P, (b + 1) * P)
                    for t in range(KX):
                        if b == 0 and t % 2 == 0:
                            pe.wait_ge(a_o2h, nth(i, 4, t // 2 + 1))
                            pe.wait_ge(d_o2l, nth(i, 4, t // 2 + 1))
                        for n, (a, w) in enumerate(((high, wo_h), (low, wo_h), (high, wo_l))):
                            last = pe.matmul(ps[:, 4, b * D:(b + 1) * D], a[:, t, rows], w[:, t, :],
                                             start=t == 0 and n == 0, stop=t == KX - 1 and n == 2)
                last.then_inc(pe_wo, 1)

            pe.wait_ge(x_loaded, 16)
            transposes(x_in, 3, 0, pe_xt)
            queries_keys(0)
            self_values(0)
            attention(0, True, None)
            attention(1, False, 0, first_f=True)
            with pe.Fori(2, B - 1) as i:
                attention(i, False, i - 1)
            attention(B - 1, False, B - 2, more=False)
            transposed_x2(B - 1)
            for u in range(4):
                layer0(B - 1, u, False)
            for m in range(KF):
                layer1(B - 1, m)
            for b in range(TB):
                layer2(B - 1, b)


_INS = ["x", "ctx_1024", "L0_attn_w_qkv", "L0_attn_b_qkv", "L0_attn_w_proj", "L0_attn_b_proj", "L0_xattn_w_q",
        "L0_xattn_w_k", "L0_xattn_w_v", "L0_xattn_w_o", "L0_ffn_k0", "L0_ffn_k1", "L0_ffn_k2", "L0_ffn_s0",
        "L0_ffn_s1", "L0_ffn_s2"]


def kernel(**inputs):
    import numpy as _np
    import concourse.bacc as _bacc
    from concourse import mybir as _mybir
    from concourse.bass_utils import run_bass_kernel_spmd as _run

    nc = _bacc.Bacc("TRN2", target_bir_lowering=False, num_devices=1)
    arrays, args = {}, []
    for name in _INS:
        a = _np.ascontiguousarray(inputs[name])
        arrays[f"in_{name}"] = a
        args.append(nc.dram_tensor(f"in_{name}", a.shape, _mybir.dt.from_np(a.dtype), kind="ExternalInput").ap())
    shape = tuple(inputs["x"].shape)
    args.append(nc.dram_tensor("out_0", shape, _mybir.dt.float32, kind="ExternalOutput").ap())
    decoder_layer(nc, *args)
    r = _run(nc, [arrays], core_ids=[0])
    return r.results[0]["out_0"]
```

```python
from contextlib import ExitStack

import concourse.bass as bass
from concourse import mybir

F32 = mybir.dt.float32
F32R = mybir.dt.float32r
F16 = mybir.dt.float16
BF16 = mybir.dt.bfloat16
U8 = mybir.dt.uint8
ALU = mybir.AluOpType
ACT = mybir.ActivationFunctionType
AX_X = mybir.AxisListType.X

P = 128
MASKED = -1e30
LOWEST = -3e38
EPS = 1e-5


def nth(i, per, k):
    return i * per + k


def decoder_layer(nc, x, ctx, w_qkv, b_qkv, w_proj, b_proj, w_q, w_k, w_v, w_o, k0, k1, k2, s0, s1, s2, out):
    B, S, D = x.shape
    SK = ctx.shape[1]
    H = 16
    HD = D // H
    XD = w_q.shape[1] // H
    F = k1.shape[0]
    KD = D // P
    TB = S // P
    NP = H // 2
    KX = w_q.shape[1] // P
    KF = F // P
    R1_SCALE = 1.0 / 16
    SELF_SCALE = float(HD) ** -0.5
    CROSS_SCALE = float(XD) ** -0.5
    ROW_M = 3 * HD
    KST = ROW_M + 1

    with ExitStack() as stack:
        def sb(name, shape, dt):
            return stack.enter_context(nc.sbuf_tensor(name, shape, dt))

        def sem(name):
            return stack.enter_context(nc.semaphore(name))

        wqkv_h = sb("wqkv_h", [P, KD, 3 * D], F32R)
        wqkv_l = sb("wqkv_l", [P, KD, 3 * D], F32R)
        wp_h = sb("wp_h", [P, KD, D], F32R)
        wp_l = sb("wp_l", [P, KD, D], F32R)
        wq_h = sb("wq_h", [P, KD, H * XD], F32R)
        wq_l = sb("wq_l", [P, KD, H * XD], F32R)
        wk = sb("wk", [P, KD, H * XD], F32)
        wv = sb("wv", [P, KD, H * XD], F32)
        wo_h = sb("wo_h", [P, KX, D], F32R)
        wo_l = sb("wo_l", [P, KX, D], F32R)
        w0 = sb("w0", [P, KD, F], F16)
        w1 = sb("w1", [P, KF, F], F16)
        w2 = sb("w2", [P, KF, D], F16)
        bias_qk = sb("bias_qk", [P, 2 * KD], F32)
        bias_v = sb("bias_v", [P, TB, D], F32)
        bias_p = sb("bias_p", [P, TB, D], F32)
        ident = sb("ident", [P, P], F32)
        causal = sb("causal", [P, 3 * P], BF16)
        head_row = sb("head_row", [P, 4, 4, SK + 1], F32R)
        sum_col = sb("sum_col", [SK, 4, 32], F32)
        minus_half = sb("minus_half", [P, TB], F32)
        scal = sb("scal", [P, 3], F32)
        sgn = sb("sgn", [P, 2], F32)
        tmp2 = sb("tmp2", [P, 2], F32)
        ffn_coef = sb("ffn_coef", [P, 4], F32)
        x_in = sb("x_in", [P, TB, D], F32)
        xb = sb("xb", [P, TB, D], F32)
        xt_h = sb("xt_h", [P, KD, S], F32R)
        xt_l = sb("xt_l", [P, KD, S], F32R)
        low = sb("low", [P, KX, S], F32R)
        q2_l = low
        high = sb("high", [P, KX, S], F32R)
        q2_h = high
        q_st = sb("q_st", [P, NP, S], F32R)
        k_st = sb("k_st", [P, NP, S], F32R)
        v = sb("v", [P, TB, H, 2 * HD], F32)
        probs = sb("probs", [P, 4, 512], F32)
        probs_flat = probs[:].rearrange("p a b -> p (a b)")
        pr = probs_flat[:, 0:2 * 768].rearrange("p (n a b) -> p n a b", n=2, a=2)
        qk_h = probs_flat[:, 0:4 * S].bitcast(F32R).rearrange("p (m t) -> p m t", m=4)
        qk_l = probs_flat[:, 4 * S:8 * S].bitcast(F32R).rearrange("p (m t) -> p m t", m=4)
        o_h = sb("o_h", [P, KD, S], F32R)
        o_l = sb("o_l", [P, KD, S], F32R)
        x1 = sb("x1", [P, TB, D], F32)
        c_in = sb("c_in", [SK, D], F32)
        ct = sb("ct", [P, KD, SK + 1], F32)
        kbd_h = sb("kbd_h", [P, KX, 2, P], F32R)
        k2_l = sb("k2_l", [P, KX, SK + 1], F32R)
        v2 = sb("v2", [SK, H * XD], F32)
        o2 = sb("o2", [P, KX, S], F32)
        o_raw = o2[:, 0:4, :]
        o_c = o2[:, 4:6, :]
        s_c = o2[:, 6:8, :]
        inv_l = sb("inv_l", [P, S], F32R)
        x2 = sb("x2", [P, TB, D], F32)
        x2t_h = sb("x2t_h", [P, KD, S], F16)
        x2t_l = sb("x2t_l", [P, KD, S], F16)
        r0_h = sb("r0_h", [P, KF, S], F16)
        r0_l = sb("r0_l", [P, KF, S], F16)
        r1_h = sb("r1_h", [P, KF, S], F16)
        r1_l = sb("r1_l", [P, KF, S], F16)
        y3 = sb("y3", [P, TB, D], F32)
        junk = sb("junk", [P, 2, 3 * P], BF16)
        row_max = sb("row_max", [P, TB, H], F32)
        row_max2 = sb("row_max2", [P, TB, P], F32)
        inv_s = row_max2[:].rearrange("p b h -> p (b h)")
        head_rows = sb("head_rows", [P, S], F32R)
        neg_max = head_rows[0:H, :]
        neg_max2 = head_rows
        inv_h = head_rows
        stats = sb("stats", [P, 3, TB, 6], F32)
        mv = sb("mv", [P, 3, TB, 2], F32)
        var_eps = sb("var_eps", [P, 3, TB], F32)
        rstd = sb("rstd", [P, 3, TB], F32)

        ps = stack.enter_context(nc.psum_tensor("ps", [P, 8, 512], F32))

        w_in = [sem(f"w_in{n}") for n in range(4)]
        wkv_in = sem("wkv_in")
        kb_in = sem("kb_in")
        small_in = sem("small_in")
        x_loaded = sem("x_loaded")
        c_loaded = sem("c_loaded")
        q_stacked = sem("q_stacked")
        k_stacked = sem("k_stacked")
        max_stacked = sem("max_stacked")
        o_packed = [sem(f"o_packed{m}") for m in range(KD)]
        stored = sem("stored")
        const_pool = sem("const_pool")
        const_dve = sem("const_dve")
        w_high = sem("w_high")
        w_low = sem("w_low")
        w_bin = sem("w_bin")
        coef = sem("coef")
        pe_xt, pe_qk, pe_v, pe_x2t, pe_ct, pe_k2, pe_v2 = (sem("pe_" + n) for n in "xt qk v x2t ct k2 v2".split())
        pe_sq, pe_mt, pe_st, pe_pv, pe_pj, pe_x1t = (sem("pe_" + n) for n in "sq mt st pv pj x1t".split())
        pe_q2, pe_sq2, pe_mt2, pe_st2, pe_pv2, pe_iv, pe_wo = (
            sem("pe_" + n) for n in "q2 sq2 mt2 st2 pv2 iv wo".split())
        pe_sum = sem("pe_sum")
        pe_z0, pe_z1, pe_z2 = (sem("pe_" + n) for n in "z0 z1 z2".split())
        a_xt, a_qk, a_x2t, a_ct, a_k2, a_v2, a_nm, a_p, a_o, a_oh = (
            sem("a_" + n) for n in "xt qk x2t ct k2 v2 nm p o oh".split())
        a_x1t, a_q2, a_nm2, a_p2, a_o2, a_ih, a_o2h, a_r0, a_r1, a_y3 = (
            sem("a_" + n) for n in "x1t q2 nm2 p2 o2 ih o2h r0 r1 y3".split())
        d_xt, d_qk, d_v, d_x2t, d_k2, d_mx, d_rc, d_on, d_ol, d_y1, d_x1, d_x1t, d_q2, d_mx2, d_is, d_il = (
            sem("d_" + n) for n in "xt qk v x2t k2 mx rc on ol y1 x1 x1t q2 mx2 is il".split())
        d_o2, d_o2l, d_y2, d_x2, d_r0, d_r1, d_y3, d_out = (
            sem("d_" + n) for n in "o2 o2l y2 x2 r0 r1 y3 out".split())
        d_bn = [sem(f"d_bn{n}") for n in range(3)]
        d_ag = [sem(f"d_ag{n}") for n in range(3)]
        g_xb, g_p = sem("g_xb"), sem("g_p")
        passed_dve, passed_pool = sem("passed_dve"), sem("passed_pool")
        g_ve = [sem(f"g_ve{n}") for n in range(3)]
        g_rs = [sem(f"g_rs{n}") for n in range(3)]

        x_rows = x.rearrange("b s d -> (b s) d")
        ctx_rows = ctx.rearrange("b s d -> (b s) d")
        out_rows = out.rearrange("b s d -> (b s) d")

        def column_pieces(n, stage, dst):
            if n:
                return [(stage, dst[:])]
            pieces = [(stage[:, :, 2 * D:], dst[:, :, 2 * D:])]
            for kk in range(KD):
                for m in range(2 * KD):
                    src = stage[:, kk, (m // 2) * D:(m // 2 + 1) * D].rearrange("p (n e d) -> p e d n", e=2, d=HD)
                    pieces.append((src[:, m % 2], dst[:, kk, m * P:(m + 1) * P].rearrange("p (d n) -> p d n", n=NP)))
            return pieces

        qk_d = nc.dram_tensor("qk_scratch", [2, P, 2 * KD, S], F32, kind="Internal").ap()
        qk_saved = sem("qk_saved")

        block = stack.enter_context(nc.Block())

        kb0 = r0_h[:].rearrange("p a b -> p (a b)").bitcast(U8).rearrange("p (k n) -> p k n", k=2 * KD)
        kb2 = r0_l[:].rearrange("p a b -> p (a b)").bitcast(U8)[:, 0:KF * D].rearrange("p (k n) -> p k n", k=KF)
        kb1 = [half[:].rearrange("p a b -> p (a b)").bitcast(U8).rearrange("p (k n) -> p k n", k=KF // 2)
               for half in (r1_h, r1_l)]
        o2_flat = o2[:].rearrange("p a b -> p (a b)")
        stage_qkv = o2_flat[:, 0:KD * 3 * D].rearrange("p (k n) -> p k n", k=KD)
        stage_p = o2_flat[:, KD * 3 * D:].rearrange("p (k n) -> p k n", k=KD)
        stage_q = o2_flat.rearrange("p (k n) -> p k n", k=KD)
        stage_o = o2[:]
        split = ((stage_qkv, wqkv_h, wqkv_l), (stage_p, wp_h, wp_l), (stage_q, wq_h, wq_l), (stage_o, wo_h, wo_l))

        @block.sync
        def _(sp):
            sp.dma_start(x_in[:], x[0].rearrange("(b p) d -> p b d", p=P)).then_inc(x_loaded, 16)
            sp.dma_start(c_in[:], ctx[0]).then_inc(c_loaded, 16)
            sp.dma_start(stage_qkv, w_qkv.rearrange("(k p) n -> p k n", p=P)).then_inc(w_in[0], 16)
            sp.dma_start(stage_p, w_proj.rearrange("(k p) n -> p k n", p=P)).then_inc(w_in[1], 16)
            for m in range(2 * KD):
                src = b_qkv[(m // 2) * D:(m // 2 + 1) * D].rearrange("(p e d) -> e d p", e=2, d=HD)[m % 2]
                sp.dma_start(bias_qk[:, m:m + 1], src, allow_slow_non_contiguous=True).then_inc(small_in, 16)
            for b in range(TB):
                sp.dma_start(bias_v[:, b, :], b_qkv[2 * D:3 * D].partition_broadcast(P)).then_inc(small_in, 16)
                sp.dma_start(bias_p[:, b, :], b_proj.partition_broadcast(P)).then_inc(small_in, 16)
            for n, s in enumerate((s0, s1, s2)):
                sp.dma_start(scal[:, n:n + 1], s.partition_broadcast(P)).then_inc(small_in, 16)
            sp.dma_start(kb0, k0.rearrange("(k p) n -> p k n", p=P)).then_inc(kb_in, 16)
            sp.dma_start(kb2, k2.rearrange("(k p) n -> p k n", p=P)).then_inc(kb_in, 16)
            for n in range(2):
                sp.dma_start(kb1[n], k1[n * F // 2:(n + 1) * F // 2].rearrange("(k p) n -> p k n", p=P)).then_inc(kb_in, 16)
            sp.dma_start(wk[:], w_k.rearrange("(k p) n -> p k n", p=P)).then_inc(wkv_in, 16)
            sp.dma_start(wv[:], w_v.rearrange("(k p) n -> p k n", p=P)).then_inc(wkv_in, 16)
            sp.wait_ge(w_low, 2)
            sp.dma_start(stage_q, w_q.rearrange("(k p) n -> p k n", p=P)).then_inc(w_in[2], 16)

            def load(j):
                sp.wait_ge(pe_xt, nth(j, 1, 0))
                sp.wait_ge(g_xb, nth(j, 1, 0))
                sp.wait_ge(pe_ct, nth(j, 1, 0))
                sp.dma_start(x_in[:], x_rows[bass.ds(j * S, S), :].rearrange("(b p) d -> p b d", p=P))\
                  .then_inc(x_loaded, 16)
                sp.dma_start(c_in[:], ctx_rows[bass.ds(j * SK, SK), :]).then_inc(c_loaded, 16)

            def head_stacks(j):
                sp.wait_ge(a_qk, nth(j, 4, 4))
                sp.dma_start(qk_d[0], qk_h.bitcast(F32)).then_inc(qk_saved, 16)
                sp.wait_ge(d_qk, nth(j, 4, 4))
                sp.dma_start(qk_d[1], qk_l.bitcast(F32)).then_inc(qk_saved, 16)
                sp.wait_ge(qk_saved, nth(j, 32, 32))
                for dst, at, both, one, done in ((q_st, 0, HD, 0, q_stacked), (k_st, KD, 0, 2 * HD, k_stacked)):
                    for e in range(2):
                        src = qk_d[:, :, at + e, :].rearrange("a (d p) t -> (a d) p t", p=NP)
                        r = 64 * e + both
                        sp.dma_start(dst[r:r + 2 * HD, :, :].bitcast(F32), src).then_inc(done, 16)
                        r = 64 * e + one
                        sp.dma_start(dst[r:r + HD, :, :].bitcast(F32), src[0:HD]).then_inc(done, 16)

            def stack_max(j):
                sp.wait_ge(a_nm, nth(j, 1, 1))
                sp.wait_ge(q_stacked, nth(j, 64, 64))
                for e in range(2):
                    sp.dma_start(q_st[64 * e + ROW_M:64 * e + ROW_M + 1, :, :].bitcast(F32),
                                 neg_max[e::2, :].bitcast(F32)).then_inc(max_stacked, 16)

            def attention(i, g, more=True):
                if more:
                    load(i + 1)
                for m in range(KD):
                    sp.wait_ge(a_o, nth(i, 2, m + 1))
                    for part, dst in ((1, s_c), (0, o_c)):
                        for e in range(2):
                            sp.dma_start(dst[64 * e:64 * e + 64, m, :], o_raw[part::2, 2 * m + e, :])\
                              .then_inc(o_packed[m], 16)
                if more:
                    head_stacks(i + 1)
                if g is not None:
                    store(g)
                if more:
                    stack_max(i + 1)

            def store(f):
                sp.wait_ge(d_out, nth(f, 2, 2))
                sp.dma_start(out_rows[bass.ds(f * S, S), :].rearrange("(b p) d -> p b d", p=P), y3[:])\
                  .then_inc(stored, 16)

            head_stacks(0)
            sp.wait_ge(w_low, 3)
            sp.dma_start(stage_o, w_o.rearrange("(k p) n -> p k n", p=P)).then_inc(w_in[3], 16)
            stack_max(0)
            attention(0, None)
            attention(1, None)
            with sp.Fori(2, B - 1) as i:
                attention(i, i - 2)
            attention(B - 1, B - 3, more=False)
            store(B - 2)
            store(B - 1)
            sp.wait_ge(stored, 16 * B)

        @block.gpsimd
        def _(pool):
            pool.memset(ident[:], 0.0).then_inc(const_pool, 1)
            pool.memset(causal[:], 0.0).then_inc(const_pool, 1)
            pool.memset(head_row[:].bitcast(F32), 1.0).then_inc(const_pool, 1)
            pool.wait_ge(const_pool, 3)
            pool.affine_select(out=ident[:], in_=ident[:], compare_op=ALU.not_equal, fill=1.0, base=0,
                               pattern=[[-1, P]], channel_multiplier=1).then_inc(const_pool, 1)
            for c in (0, 2):
                tri = causal[:, c * P:(c + 1) * P]
                pool.affine_select(out=tri, in_=tri, compare_op=ALU.is_ge, fill=MASKED, base=0,
                                   pattern=[[-1, P]], channel_multiplier=1).then_inc(const_pool, 1)
            pool.affine_select(out=head_row[:], in_=head_row[:], compare_op=ALU.is_equal, fill=0.0, base=0,
                               pattern=[[-1, 4], [-32, 4], [0, SK + 1]], channel_multiplier=1).then_inc(const_pool, 1)
            pool.memset(minus_half[:], -0.5).then_inc(const_pool, 1)
            pool.memset(sum_col[:], 0.0).then_inc(const_pool, 1)
            pool.wait_ge(const_pool, 9)
            for g in range(4):
                pool.memset(sum_col[:, g, g:g + 1], 1.0).then_inc(const_pool, 1)
            pool.memset(sum_col[:, 0, 4:32], 1.0).then_inc(const_pool, 1)
            pool.wait_ge(const_pool, 14)
            pool.wait_ge(small_in, 16 * 11)

            def biased(j):
                pool.wait_ge(x_loaded, nth(j, 16, 16))
                pool.tensor_tensor(xb[:], x_in[:], bias_p[:], ALU.add).then_inc(g_xb, 1)

            def attention(i, f, g, more=True):
                for n in range(NP):
                    pool.wait_ge(a_p, nth(i, NP, n + 1))
                    pool.sem_inc(passed_pool, 1)
                    diag = pr[:, n % 2, :, 0:2 * P].rearrange("p a (b q) -> p a b q", b=2)
                    pool.affine_select(out=diag, in_=diag, compare_op=ALU.is_ge, fill=0.0, base=0,
                                       pattern=[[0, 2], [0, 2], [1, P]], channel_multiplier=-1).then_inc(g_p, 1)
                    if n == 0 and f is not None:
                        inverse_deviation(1, f)
                    if n == NP - 1 and g is not None:
                        inverse_deviation(2, g)
                inverse_deviation(0, i)
                if more:
                    biased(i + 1)

            def inverse_deviation(n, i):
                pool.wait_ge(d_ag[n], nth(i, 2, 2))
                pool.sem_inc(passed_pool, 1)
                pool.tensor_scalar(var_eps[:, n, :], mv[:, n, :, 1], EPS, None, ALU.add).then_inc(g_ve[n], 1)
                pool.wait_ge(g_ve[n], nth(i, 1, 1))
                pool.tensor_tensor(rstd[:, n, :], var_eps[:, n, :], minus_half[:], ALU.pow).then_inc(g_rs[n], 1)

            biased(0)
            attention(0, None, None)
            attention(1, 0, None)
            with pool.Fori(2, B - 1) as i:
                attention(i, i - 1, i - 2)
            attention(B - 1, B - 2, B - 3, more=False)
            inverse_deviation(1, B - 1)
            inverse_deviation(2, B - 2)
            inverse_deviation(2, B - 1)

        @block.scalar
        def _(act):
            def split_high(n):
                stage, high_part, _ = split[n]
                act.wait_ge(w_in[n], 16)
                for src, dst in column_pieces(n, stage, high_part):
                    last = act.activation(dst, src, ACT.Copy)
                last.then_inc(w_high, 1)

            def relu(bank, r_h, pe_z, done, f, u):
                act.wait_ge(pe_z, nth(f, 4, u + 1))
                act.activation(r_h[:, 2 * u:2 * u + 2, :], ps[:, bank, :], ACT.Relu).then_inc(done, 1)

            def transposed_x(j):
                act.wait_ge(pe_xt, nth(j, 1, 1))
                act.activation(xt_h[:], ps[:, 4, :], ACT.Copy).then_inc(a_xt, 1)
                act.wait_ge(pe_ct, nth(j, 1, 1))
                act.activation(ct[:, :, 0:SK], ps[:, 5, 0:2 * P].rearrange("p (k t) -> p k t", k=2)[:, :, 0:SK],
                               ACT.Copy).then_inc(a_ct, 1)

            def queries_keys(j, u):
                act.wait_ge(pe_qk, nth(j, 2, u + 1))
                for m in (2 * u, 2 * u + 1):
                    act.activation(qk_h[:, m, :], ps[:, 6 + u, (m % 2) * S:(m % 2 + 1) * S], ACT.Identity,
                                   bias=bias_qk[:, m:m + 1]).then_inc(a_qk, 1)

            def cross_keys(j, n):
                act.wait_ge(pe_k2, nth(j, 2, n + 1))
                src = ps[:, 4 + n, :].rearrange("p (m t) -> p m t", m=4)
                for e in range(2):
                    act.activation(kbd_h[64 * e:64 * e + 64, 4 * n:4 * n + 4, e, 0:SK],
                                   src[64 * e:64 * e + 64, :, 0:SK], ACT.Copy).then_inc(a_k2, 1)

            def negated_max(j):
                act.wait_ge(pe_mt, nth(j, 1, 1))
                act.activation(neg_max[:], ps[0:H, 4, 0:S], ACT.Copy, scale=-1.0).then_inc(a_nm, 1)

            def cross_values(j):
                for n in range(2):
                    act.wait_ge(pe_v2, nth(j, 2, n + 1))
                    act.activation(v2[:, n * 512:(n + 1) * 512], ps[0:SK, n, :], ACT.Copy).then_inc(a_v2, 1)

            def residual(f, first_f):
                act.wait_ge(d_x2, nth(f, 2, 2))
                if not first_f:
                    act.wait_ge(stored, nth(f, 16, 0))
                act.activation(y3[:], x2[:], ACT.Copy).then_inc(a_y3, 1)

            def attention(i, first, f, first_f=False, more=True):
                for n in range(NP):
                    act.wait_ge(pe_st, nth(i, NP, n + 1))
                    if n >= 2:
                        act.wait_ge(pe_pv, nth(i, NP, n - 1))
                    b = 4 + 2 * (n % 2)
                    act.activation(pr[:, n % 2, :, :], ps[:, b:b + 2, P:512], ACT.Exp, scale=SELF_SCALE)\
                       .then_inc(a_p, 1)
                    if n == 3 and not first:
                        transposed_x2(f)
                    if n == 6 and not first:
                        relu(0, r0_h, pe_z0, a_r0, f, 0)
                    if n == NP - 1 and more:
                        transposed_x(i + 1)
                    if n in (5, NP - 1):
                        m = n // (NP - 1)
                        act.wait_ge(pe_pv, nth(i, NP, 4 * m + 4))
                        act.activation(o_raw[:, 2 * m:2 * m + 2, :], ps[:, 2 + m, :], ACT.Copy).then_inc(a_o, 1)
                if not first:
                    relu(1, r0_h, pe_z0, a_r0, f, 1)
                    relu(0, r0_h, pe_z0, a_r0, f, 2)
                act.wait_ge(d_on, nth(i, 2, 1))
                act.activation(o_h[:, 0, :], o_c[:, 0, :], ACT.Copy).then_inc(a_oh, 1)
                if not first:
                    relu(1, r0_h, pe_z0, a_r0, f, 3)
                if more:
                    queries_keys(i + 1, 0)
                    queries_keys(i + 1, 1)
                act.wait_ge(d_on, nth(i, 2, 2))
                act.activation(o_h[:, 1, :], o_c[:, 1, :], ACT.Copy).then_inc(a_oh, 1)
                if not first:
                    relu(0, r1_h, pe_z1, a_r1, f, 0)
                    relu(1, r1_h, pe_z1, a_r1, f, 1)
                act.wait_ge(pe_x1t, nth(i, 1, 1))
                act.activation(xt_h[:], ps[:, 3, :], ACT.Copy).then_inc(a_x1t, 1)
                for u in range(4):
                    act.wait_ge(pe_q2, nth(i, 4, u + 1))
                    act.activation(q2_h[:, 2 * u:2 * u + 2, :], ps[:, 6 + u % 2, :], ACT.Copy).then_inc(a_q2, 1)
                    if u == 2 and not first:
                        relu(0, r1_h, pe_z1, a_r1, f, 2)
                act.wait_ge(pe_mt2, nth(i, 1, 1))
                act.activation(neg_max2[:], ps[:, 2, 0:S], ACT.Copy, scale=-1.0).then_inc(a_nm2, 1)
                if not first:
                    relu(1, r1_h, pe_z1, a_r1, f, 3)
                    residual(f, first_f)
                if more:
                    act.wait_ge(qk_saved, nth(i + 1, 32, 32))
                for u in range(5):
                    if u < 4:
                        for e in range(2):
                            act.wait_ge(pe_st2, nth(i, 8, 2 * u + e + 1))
                            if u >= 2:
                                act.wait_ge(pe_pv2, nth(i, 4, u - 1))
                            act.activation(probs[0:SK, 2 * (u % 2) + e, :], ps[0:SK, 4 + 2 * (u % 2) + e, :],
                                           ACT.Exp, scale=CROSS_SCALE).then_inc(a_p2, 1)
                    if u == 4 and more:
                        cross_keys(i + 1, 0)
                    if u >= 1:
                        act.wait_ge(pe_pv2, nth(i, 4, u))
                        act.activation(o2[:, 2 * u - 2:2 * u, :], ps[:, 2, :], ACT.Copy).then_inc(a_o2, 1)
                act.wait_ge(d_is, nth(i, 1, 1))
                act.activation(inv_h[:], inv_s, ACT.Copy).then_inc(a_ih, 1)
                if more:
                    cross_keys(i + 1, 1)
                for u in range(4):
                    if u == 2 and more:
                        negated_max(i + 1)
                    act.wait_ge(d_o2, nth(i, 4, u + 1))
                    act.activation(high[:, 2 * u:2 * u + 2, :], o2[:, 2 * u:2 * u + 2, :], ACT.Copy)\
                       .then_inc(a_o2h, 1)
                if more:
                    cross_values(i + 1)

            def transposed_x2(f):
                act.wait_ge(pe_x2t, nth(f, 1, 1))
                act.activation(x2t_h[:], ps[:, 0, :], ACT.Copy).then_inc(a_x2t, 1)

            split_high(0)
            split_high(1)
            transposed_x(0)
            act.wait_ge(small_in, 16 * 11)
            queries_keys(0, 0)
            queries_keys(0, 1)
            cross_keys(0, 0)
            cross_keys(0, 1)
            split_high(2)
            split_high(3)
            negated_max(0)
            cross_values(0)
            attention(0, True, None)
            attention(1, False, 0, first_f=True)
            with act.Fori(2, B - 1) as i:
                attention(i, False, i - 1)
            attention(B - 1, False, B - 2, more=False)
            transposed_x2(B - 1)
            for u in range(4):
                relu(u % 2, r0_h, pe_z0, a_r0, B - 1, u)
            residual(B - 1, False)
            for u in range(4):
                relu(u % 2, r1_h, pe_z1, a_r1, B - 1, u)

        @block.vector
        def _(dve):
            dve.memset(k_st[:].bitcast(F32), 1.0).then_inc(const_dve, 1)
            dve.memset(v[:], 1.0).then_inc(const_dve, 1)
            dve.memset(kbd_h[:].bitcast(F32), 0.0).then_inc(const_dve, 1)
            dve.memset(row_max2[:], 0.0).then_inc(const_dve, 1)

            def split_low(n):
                stage, high_part, low_part = split[n]
                dve.wait_ge(w_high, n + 1)
                for (src, dst), (_, top) in zip(column_pieces(n, stage, low_part), column_pieces(n, stage, high_part)):
                    last = dve.tensor_tensor(dst, src, top.bitcast(F32), ALU.subtract)
                last.then_inc(w_low, 1)

            def layer_norm_stats(n, y, i):
                if n == 2:
                    dve.wait_ge(d_y3, nth(i, 2, 2))
                for b in range(TB):
                    dve.bn_stats(stats[:, n, b, :], y[:, b, :]).then_inc(d_bn[n], 1)
                for b in range(TB):
                    dve.wait_ge(d_bn[n], nth(i, 2, b + 1))
                    dve.sem_inc(passed_dve, 1)
                    dve.bn_aggr(mv[:, n, b, :], stats[:, n, b, :]).then_inc(d_ag[n], 1)

            def layer_norm_apply(n, dst, y, done, i):
                dve.wait_ge(g_rs[n], nth(i, 1, 1))
                for b in range(TB):
                    dve.tensor_scalar(dst[:, b, :], y[:, b, :], mv[:, n, b, 0:1], rstd[:, n, b:b + 1],
                                      ALU.subtract, ALU.mult).then_inc(done, 1)

            def relu_low(bank, r_h, r_l, high_done, done, f, u):
                dve.wait_ge(high_done, nth(f, 4, u + 1))
                dve.scalar_tensor_tensor(r_l[:, 2 * u:2 * u + 2, :], ps[:, bank, :].rearrange("p (a t) -> p a t", a=2),
                                         0.0, r_h[:, 2 * u:2 * u + 2, :], ALU.max, ALU.subtract).then_inc(done, 1)

            def self_max(i, h):
                dve.wait_ge(pe_sq, nth(i, H, h + 1))
                bank = h % 2
                for b, keys in enumerate((slice(0, P), slice(S, 2 * S))):
                    k = 2 * h + b
                    width = (b + 1) * P
                    if not (isinstance(i, int) and i == 0 and k < 4):
                        dve.wait_ge(d_mx, nth(i, 2 * H, k - 3))
                    dve.sem_inc(passed_dve, 1)
                    dve.tensor_tensor_reduce(out=junk[:, h % 2, b * P:b * P + width], in0=ps[:, bank, keys],
                                             in1=causal[:, b * P:b * P + width], scale=1.0, scalar=LOWEST,
                                             op0=ALU.add, op1=ALU.max, accum_out=row_max[:, b, h:h + 1])\
                       .then_inc(d_mx, 1)

            def transposed_x(j):
                dve.wait_ge(a_xt, nth(j, 1, 1))
                dve.tensor_tensor(xt_l[:].rearrange("p a b -> p (a b)"), ps[:, 4, :],
                                  xt_h[:].rearrange("p a b -> p (a b)").bitcast(F32), ALU.subtract).then_inc(d_xt, 1)

            def queries_keys(j, m):
                dve.wait_ge(a_qk, nth(j, 4, 2 * (m // 2) + 2))
                dve.scalar_tensor_tensor(qk_l[:, m, :], ps[:, 6 + m // 2, (m % 2) * S:(m % 2 + 1) * S],
                                         bias_qk[:, m:m + 1], qk_h[:, m, :].bitcast(F32),
                                         ALU.add, ALU.subtract).then_inc(d_qk, 1)

            def self_values(j):
                dve.wait_ge(pe_v, nth(j, 1, 1))
                dve.tensor_tensor(v[:, :, :, 0::2].rearrange("p b h d -> p (b h) d"),
                                  ps[:, 5, :].rearrange("p (m d) -> p m d", d=HD),
                                  bias_v[:].rearrange("p b (h d) -> p (b h) d", d=HD), ALU.add).then_inc(d_v, 1)

            def self_output(i, m):
                dve.wait_ge(o_packed[m], nth(i, 64, 64))
                dve.reciprocal(s_c[:, m, :], s_c[:, m, :]).then_inc(d_rc, 1)
                dve.wait_ge(d_rc, nth(i, 2, m + 1))
                dve.tensor_tensor(o_c[:, m, :], o_c[:, m, :], s_c[:, m, :], ALU.mult).then_inc(d_on, 1)

            def self_output_low(i, m):
                dve.wait_ge(a_oh, nth(i, 2, m + 1))
                dve.tensor_tensor(o_l[:, m, :], o_c[:, m, :], o_h[:, m, :].bitcast(F32), ALU.subtract).then_inc(d_ol, 1)

            def cross_keys(j, n):
                for e in range(2):
                    dve.wait_ge(a_k2, nth(j, 4, 2 * n + e + 1))
                    rows = slice(64 * e, 64 * e + 64)
                    dve.tensor_tensor(k2_l[rows, 4 * n:4 * n + 4, 0:SK],
                                      ps[:, 4 + n, :].rearrange("p (m t) -> p m t", m=4)[rows, :, 0:SK],
                                      kbd_h[rows, 4 * n:4 * n + 4, e, 0:SK].bitcast(F32), ALU.subtract)\
                       .then_inc(d_k2, 1)

            def attention(i, first, f, g, more=True):
                if not first:
                    layer_norm_apply(1, x2, x2, d_x2, f)
                if g is not None:
                    ffn_sum(g, 0)
                if not first:
                    transposed_x2(f)
                if g is not None:
                    ffn_sum(g, 1)
                    layer_norm_stats(2, y3, g)
                if not first:
                    relu_low(0, r0_h, r0_l, a_r0, d_r0, f, 0)
                if more:
                    transposed_x(i + 1)
                if not first:
                    relu_low(1, r0_h, r0_l, a_r0, d_r0, f, 1)
                self_output(i, 0)
                if not first:
                    relu_low(0, r0_h, r0_l, a_r0, d_r0, f, 2)
                self_output_low(i, 0)
                if not first:
                    relu_low(1, r0_h, r0_l, a_r0, d_r0, f, 3)
                self_output(i, 1)
                self_output_low(i, 1)
                if more:
                    for m in range(4):
                        queries_keys(i + 1, m)
                    self_values(i + 1)
                dve.wait_ge(pe_pj, nth(i, 1, 1))
                dve.tensor_tensor(x1[:].rearrange("p a b -> p (a b)"), ps[:, 4, :],
                                  xb[:].rearrange("p a b -> p (a b)"), ALU.add).then_inc(d_y1, 1)
                dve.wait_ge(d_y1, nth(i, 1, 1))
                layer_norm_stats(0, x1, i)
                if not first:
                    relu_low(0, r1_h, r1_l, a_r1, d_r1, f, 0)
                layer_norm_apply(0, x1, x1, d_x1, i)
                if not first:
                    relu_low(1, r1_h, r1_l, a_r1, d_r1, f, 1)
                dve.wait_ge(a_x1t, nth(i, 1, 1))
                dve.tensor_tensor(xt_l[:].rearrange("p a b -> p (a b)"), ps[:, 3, :],
                                  xt_h[:].rearrange("p a b -> p (a b)").bitcast(F32), ALU.subtract).then_inc(d_x1t, 1)
                if g is not None:
                    ffn_norm(g)
                for u in range(5):
                    if u < 4:
                        dve.wait_ge(a_q2, nth(i, 4, u + 1))
                        dve.tensor_tensor(q2_l[:, 2 * u:2 * u + 2, :].rearrange("p a b -> p (a b)"), ps[:, 6 + u % 2, :],
                                          q2_h[:, 2 * u:2 * u + 2, :].rearrange("p a b -> p (a b)").bitcast(F32),
                                          ALU.subtract).then_inc(d_q2, 1)
                    if u >= 1:
                        for t in (2 * u - 2, 2 * u - 1):
                            dve.wait_ge(pe_sq2, nth(i, KX, t + 1))
                            at = 64 * (t % 2) + t // 2
                            dve.tensor_reduce(row_max2[:, :, at:at + 33:32],
                                              ps[:, 4 + t % 2, :].rearrange("p (b e k) -> p b e k", b=2, e=2)[:, :, :, 0:SK],
                                              AX_X, ALU.max).then_inc(d_mx2, 1)
                    if u >= 3 and not first:
                        relu_low((u - 1) % 2, r1_h, r1_l, a_r1, d_r1, f, u - 1)
                if more:
                    for h in range(H):
                        self_max(i + 1, h)
                    cross_keys(i + 1, 0)
                dve.wait_ge(pe_sum, nth(i, 1, 1))
                dve.reciprocal(inv_s, ps[:, 3, 0:S]).then_inc(d_is, 1)
                dve.wait_ge(a_ih, nth(i, 1, 1))
                dve.tensor_tensor(inv_l[:], inv_s, inv_h[:].bitcast(F32), ALU.subtract).then_inc(d_il, 1)
                for u in range(5):
                    if u < 4:
                        dve.wait_ge(pe_iv, nth(i, 4, u + 1))
                        dve.wait_ge(a_o2, nth(i, 4, u + 1))
                        o2u = o2[:, 2 * u:2 * u + 2, :].rearrange("p a b -> p (a b)")
                        dve.tensor_tensor(o2u, o2u, ps[:, 2 + u % 2, :], ALU.mult).then_inc(d_o2, 1)
                    if u == 1 and more:
                        cross_keys(i + 1, 1)
                    if u >= 1:
                        dve.wait_ge(a_o2h, nth(i, 4, u))
                        dve.tensor_tensor(low[:, 2 * u - 2:2 * u, :], o2[:, 2 * u - 2:2 * u, :],
                                          high[:, 2 * u - 2:2 * u, :].bitcast(F32), ALU.subtract).then_inc(d_o2l, 1)
                dve.wait_ge(pe_wo, nth(i, 1, 1))
                dve.tensor_tensor(x2[:], ps[:, 6:8, 0:D], x1[:], ALU.add).then_inc(d_y2, 1)
                dve.wait_ge(d_y2, nth(i, 1, 1))
                layer_norm_stats(1, x2, i)

            def transposed_x2(f):
                dve.wait_ge(a_x2t, nth(f, 1, 1))
                dve.tensor_tensor(x2t_l[:].rearrange("p a b -> p (a b)"), ps[:, 0, :],
                                  x2t_h[:].rearrange("p a b -> p (a b)"), ALU.subtract).then_inc(d_x2t, 1)

            def ffn_sum(f, b):
                dve.wait_ge(a_y3, nth(f, 1, 1))
                dve.wait_ge(pe_z2, nth(f, 2, b + 1))
                dve.scalar_tensor_tensor(y3[:, b, :], ps[:, b, 0:D], ffn_coef[:, 3:4], y3[:, b, :],
                                         ALU.mult, ALU.add).then_inc(d_y3, 1)

            def ffn_norm(f):
                layer_norm_apply(2, y3, y3, d_out, f)

            split_low(0)
            split_low(1)
            dve.wait_ge(const_dve, 4)
            transposed_x(0)
            dve.wait_ge(small_in, 16 * 11)
            dve.tensor_scalar(tmp2[:], scal[:, 0:2], 0.0, None, ALU.is_lt).then_inc(coef, 1)
            dve.wait_ge(coef, 1)
            dve.scalar_tensor_tensor(sgn[:], scal[:, 0:2], 0.0, tmp2[:], ALU.is_gt, ALU.subtract).then_inc(coef, 1)
            dve.wait_ge(coef, 2)
            dve.tensor_scalar(ffn_coef[:, 0:1], sgn[:, 0:1], 2.0, None, ALU.mult).then_inc(coef, 1)
            dve.tensor_scalar(ffn_coef[:, 1:2], sgn[:, 1:2], 2.0 * R1_SCALE, None, ALU.mult).then_inc(coef, 1)
            dve.tensor_scalar(ffn_coef[:, 2:3], sgn[:, 1:2], -R1_SCALE, None, ALU.mult).then_inc(coef, 1)
            dve.tensor_tensor(tmp2[:], scal[:, 0:2], sgn[:], ALU.mult).then_inc(coef, 1)
            dve.wait_ge(coef, 6)
            dve.scalar_tensor_tensor(ffn_coef[:, 3:4], tmp2[:, 0:1], tmp2[:, 1:2], scal[:, 2:3],
                                     ALU.mult, ALU.mult).then_inc(coef, 1)
            dve.wait_ge(coef, 7)
            dve.tensor_scalar(ffn_coef[:, 3:4], ffn_coef[:, 3:4], 4.0 / R1_SCALE, None, ALU.mult).then_inc(coef, 1)
            dve.wait_ge(coef, 8)
            for m in range(4):
                queries_keys(0, m)
            self_values(0)
            cross_keys(0, 0)
            cross_keys(0, 1)
            dve.wait_ge(kb_in, 16 * 4)
            dve.tensor_tensor(w0[:], kb0[:, 0:KD, :], kb0[:, KD:2 * KD, :], ALU.subtract).then_inc(w_bin, 1)
            for n in range(2):
                dve.tensor_scalar(w1[:, n * KF // 2:(n + 1) * KF // 2, :], kb1[n], ffn_coef[:, 1:2], ffn_coef[:, 2:3],
                                  ALU.mult, ALU.add).then_inc(w_bin, 1)
            dve.tensor_scalar(w2[:], kb2, 2.0, -1.0, ALU.mult, ALU.add).then_inc(w_bin, 1)
            dve.wait_ge(w_bin, 1)
            dve.tensor_scalar(w0[:], w0[:], ffn_coef[:, 0:1], None, ALU.mult).then_inc(w_bin, 1)
            split_low(2)
            split_low(3)
            dve.wait_ge(const_pool, 14)
            for h in range(H):
                self_max(0, h)
            attention(0, True, None, None)
            attention(1, False, 0, None)
            with dve.Fori(2, B - 1) as i:
                attention(i, False, i - 1, i - 2)
            attention(B - 1, False, B - 2, B - 3, more=False)
            layer_norm_apply(1, x2, x2, d_x2, B - 1)
            ffn_sum(B - 2, 0)
            transposed_x2(B - 1)
            ffn_sum(B - 2, 1)
            layer_norm_stats(2, y3, B - 2)
            ffn_norm(B - 2)
            for u in range(4):
                relu_low(u % 2, r0_h, r0_l, a_r0, d_r0, B - 1, u)
            for u in range(4):
                relu_low(u % 2, r1_h, r1_l, a_r1, d_r1, B - 1, u)
            ffn_sum(B - 1, 0)
            ffn_sum(B - 1, 1)
            layer_norm_stats(2, y3, B - 1)
            ffn_norm(B - 1)

        @block.tensor
        def _(pe):
            pe.wait_ge(const_pool, 14)
            pe.wait_ge(const_dve, 4)

            def transposes(src, bank, i, done):
                for kk in range(KD):
                    for b in range(TB):
                        last = pe.transpose(ps[:, bank, kk * S + b * P:kk * S + (b + 1) * P],
                                            src[:, b, kk * P:(kk + 1) * P], ident[:])
                last.then_inc(done, 1)

            def weights_by_tokens(dst, w_h, w_l, cols, a_h, a_l, low_ready=None):
                for n, (w, a) in enumerate(((w_h, a_h), (w_l, a_h), (w_h, a_l))):
                    if n == 2 and low_ready:
                        pe.wait_ge(*low_ready)
                    for kk in range(KD):
                        last = pe.matmul(dst, w[:, kk, cols], a[:, kk, :], start=kk == 0 and n == 0,
                                         stop=kk == KD - 1 and n == 2)
                return last

            def tokens_by_weights(dst, a_h, a_l, b, w_h, w_l, cols):
                rows = slice(b * P, (b + 1) * P)
                for n, (a, w) in enumerate(((a_h, w_h), (a_h, w_l), (a_l, w_h))):
                    for kk in range(KD):
                        last = pe.matmul(dst, a[:, kk, rows], w[:, kk, cols], start=kk == 0 and n == 0,
                                         stop=kk == KD - 1 and n == 2)
                return last

            def layer0(f, m):
                u = m // 2
                if m == 0:
                    pe.wait_ge(a_x2t, nth(f, 1, 1))
                    pe.wait_ge(d_x2t, nth(f, 1, 1))
                if m >= 4 and m % 2 == 0:
                    pe.wait_ge(d_r0, nth(f, 4, u - 1))
                for half, x2t in enumerate((x2t_h, x2t_l)):
                    for kk in range(KD):
                        last = pe.matmul(ps[:, u % 2, (m % 2) * S:(m % 2 + 1) * S], w0[:, kk, m * P:(m + 1) * P],
                                         x2t[:, kk, :], start=half == 0 and kk == 0, stop=half == 1 and kk == KD - 1)
                if m % 2:
                    last.then_inc(pe_z0, 1)

            def layer1(f, q):
                m, part = q // 4, q % 4
                u = m // 2
                if q < 4:
                    pe.wait_ge(d_r0, nth(f, 4, max(q + 1, 3)))
                if q == 8:
                    pe.wait_ge(d_r0, nth(f, 4, 4))
                if q % 8 == 0 and u >= 2:
                    pe.wait_ge(d_r1, nth(f, 4, u - 1))
                for kk in (2 * part, 2 * part + 1):
                    dst = ps[:, u % 2, (m % 2) * S:(m % 2 + 1) * S]
                    pe.matmul(dst, w1[:, kk, m * P:(m + 1) * P], r0_h[:, kk, :], start=kk == 0, stop=False)
                    last = pe.matmul(dst, w1[:, kk, m * P:(m + 1) * P], r0_l[:, kk, :], start=False, stop=kk == KF - 1)
                if q % 8 == 7:
                    last.then_inc(pe_z1, 1)

            def layer2(f, b, blocks=range(KF)):
                if b == 0 and blocks[0] == 0:
                    pe.wait_ge(d_r1, nth(f, 4, 4))
                rows = slice(b * P, (b + 1) * P)
                for kk in blocks:
                    pe.matmul(ps[:, b, 0:D], r1_h[:, kk, rows], w2[:, kk, :], start=kk == 0, stop=False)
                    last = pe.matmul(ps[:, b, 0:D], r1_l[:, kk, rows], w2[:, kk, :], start=False, stop=kk == KF - 1)
                if kk == KF - 1:
                    last.then_inc(pe_z2, 1)

            def transposed_x2(f):
                pe.wait_ge(d_x2, nth(f, 2, 2))
                transposes(x2, 0, f, pe_x2t)

            def scores_by_query(i, h):
                if h >= 2:
                    pe.wait_ge(d_mx, nth(i, 2 * H, 2 * (h - 1)))
                rows = slice(64 * (h % 2), 64 * (h % 2) + ROW_M)
                for b in range(TB):
                    last = pe.matmul(ps[:, h % 2, b * S:(b + 1) * S], q_st[rows, h // 2, b * P:(b + 1) * P],
                                     k_st[rows, h // 2, :], start=True, stop=True)
                last.then_inc(pe_sq, 1)

            def scores_by_key(i, n):
                if n >= 2:
                    pe.wait_ge(a_p, nth(i, NP, n - 1))
                for e in range(2):
                    rows = slice(64 * e, 64 * e + KST)
                    for kb in (1, 0):
                        last = pe.matmul(ps[:, 4 + 2 * (n % 2) + e, (1 - kb) * S:(2 - kb) * S],
                                         k_st[rows, n, kb * P:(kb + 1) * P], q_st[rows, n, :], start=True, stop=True)
                last.then_inc(pe_st, 1)

            def values(i, n):
                pe.wait_ge(g_p, nth(i, NP, n + 1))
                for e in range(2):
                    h = 2 * n + e
                    g, j = h // 4, h % 4
                    c = (g % 2) * S
                    rows = slice(32 * j, 32 * j + 32)
                    pe.matmul(ps[rows, 2 + g // 2, c:c + S], v[:, 0, h, :], pr[:, n % 2, e, P:3 * P],
                              start=True, stop=False)
                    last = pe.matmul(ps[rows, 2 + g // 2, c + P:c + S], v[:, 1, h, :], pr[:, n % 2, e, 0:P],
                                     start=False, stop=True)
                last.then_inc(pe_pv, 1)

            def cross_scores_by_query(i, t):
                if t >= 2:
                    pe.wait_ge(d_mx2, nth(i, KX, t - 1))
                for b in range(TB):
                    last = pe.matmul(ps[:, 4 + t % 2, b * S:(b + 1) * S], q2_h[:, t, b * P:(b + 1) * P],
                                     kbd_h[:, t, :, :].rearrange("p e k -> p (e k)"), start=True, stop=True)
                last.then_inc(pe_sq2, 1)

            def cross_scores_by_key(i, u, between):
                if u >= 2:
                    pe.wait_ge(a_p2, nth(i, 8, 2 * u - 2))
                for e in range(2):
                    rows = slice(64 * e, 64 * e + 64)
                    for t in (2 * u, 2 * u + 1):
                        dst = ps[0:SK, 4 + 2 * (u % 2) + e, (t % 2) * S:(t % 2 + 1) * S]
                        pe.matmul(dst, kbd_h[:, t, e, 0:SK], q2_h[:, t, :], start=True, stop=False)
                        pe.matmul(dst, kbd_h[:, t, e, 0:SK], q2_l[:, t, :], start=False, stop=False)
                        pe.matmul(dst, k2_l[rows, t, 0:SK], q2_h[rows, t, :], start=False, stop=False)
                        last = pe.matmul(dst, head_row[:, t // 2, 2 * (t % 2) + e, 0:SK], neg_max2[:],
                                         start=False, stop=True)
                        if t % 2:
                            last.then_inc(pe_st2, 1)
                        if e or t % 2:
                            between()

            def cross_values(i, u, between):
                pe.wait_ge(a_p2, nth(i, 8, 2 * u + 2))
                for t in (2 * u, 2 * u + 1):
                    for e in range(2):
                        p = probs[0:SK, 2 * (u % 2) + e, (t % 2) * S:(t % 2 + 1) * S]
                        j = (2 * t + e) % 4
                        last = pe.matmul(ps[32 * j:32 * j + 32, 3, 0:S], sum_col[:, u, :], p,
                                         start=u == 0, stop=u == 3)
                        if u == 3 and j == 3:
                            last.then_inc(pe_sum, 1)
                        between()
                if u >= 1:
                    pe.wait_ge(a_o2, nth(i, 4, u))
                for t in (2 * u, 2 * u + 1):
                    for e in range(2):
                        p = probs[0:SK, 2 * (u % 2) + e, (t % 2) * S:(t % 2 + 1) * S]
                        last = pe.matmul(ps[64 * e:64 * e + 64, 2, (t % 2) * S:(t % 2 + 1) * S],
                                         v2[:, (2 * t + e) * XD:(2 * t + e + 1) * XD], p, start=True, stop=True)
                        if (t % 2, e) == (1, 1):
                            last.then_inc(pe_pv2, 1)
                        between()

            def transposed_inputs(j):
                pe.wait_ge(x_loaded, nth(j, 16, 16))
                transposes(x_in, 4, j, pe_xt)
                pe.wait_ge(c_loaded, nth(j, 16, 16))
                for kk in range(KD):
                    last = pe.transpose(ps[:, 5, kk * P:kk * P + SK], c_in[:, kk * P:(kk + 1) * P],
                                        ident[0:SK, 0:SK])
                last.then_inc(pe_ct, 1)

            def queries_keys(j, u):
                for m in (2 * u, 2 * u + 1):
                    last = weights_by_tokens(ps[:, 6 + m // 2, (m % 2) * S:(m % 2 + 1) * S], wqkv_h, wqkv_l,
                                             slice(m * P, (m + 1) * P), xt_h, xt_l)
                    if m % 2:
                        last.then_inc(pe_qk, 1)

            def self_values(j):
                for b in range(TB):
                    last = tokens_by_weights(ps[:, 5, b * D:(b + 1) * D], xt_h, xt_l, b, wqkv_h, wqkv_l,
                                             slice(2 * D, 3 * D))
                last.then_inc(pe_v, 1)

            def spread_inverse(i, u):
                if u >= 2:
                    pe.wait_ge(d_o2, nth(i, 4, u - 1))
                for t in (2 * u, 2 * u + 1):
                    dst = ps[:, 2 + u % 2, (t % 2) * S:(t % 2 + 1) * S]
                    seam = (2 * t + 1) * (SK + 1)
                    pair = head_row[:].rearrange("p u j k -> p (u j k)")[:, seam - XD:seam + XD]
                    pe.matmul(dst, pair, inv_h[:], start=True, stop=False)
                    last = pe.matmul(dst, pair, inv_l[:], start=False, stop=True)
                last.then_inc(pe_iv, 1)

            def cross_keys(j, n, step):
                if n == 0 and step == 0:
                    pe.wait_ge(a_ct, nth(j, 1, 1))
                m, kk = 4 * n + step // 2, step % 2
                last = pe.matmul(ps[:, 4 + n, (m % 4) * P:(m % 4) * P + SK], wk[:, kk, m * P:(m + 1) * P],
                                 ct[:, kk, 0:SK], start=kk == 0, stop=kk == KD - 1)
                if step == 7:
                    last.then_inc(pe_k2, 1)

            def cross_values_of(j, n, kk):
                last = pe.matmul(ps[0:SK, n, :], ct[:, kk, 0:SK], wv[:, kk, n * 512:(n + 1) * 512],
                                 start=kk == 0, stop=kk == KD - 1)
                if kk == KD - 1:
                    last.then_inc(pe_v2, 1)

            def transposed_max(j):
                pe.wait_ge(d_k2, nth(j, 4, 2))
                for b in range(TB):
                    last = pe.transpose(ps[0:H, 4, b * P:(b + 1) * P], row_max[:, b, :], ident[:])
                last.then_inc(pe_mt, 1)

            def layer1_until(f, q0, q1):
                if f is not None:
                    for q in range(q0, q1):
                        layer1(f, q)

            Z_PJ, Z_LN, Z_XT = 8, 18, 21
            Z_Q2 = (21, 21, 24, 26, 28)
            Z_MT = 30

            def attention(i, f, g, more=True):
                pe.wait_ge(max_stacked, nth(i, 32, 32))
                pe.wait_ge(a_nm, nth(i, 1, 1))
                pe.wait_ge(d_k2, nth(i, 4, 4))
                pe.wait_ge(a_v2, nth(i, 2, 2))
                for n in range(NP + 1):
                    if n == 1 and f is not None:
                        pe.wait_ge(d_y2, nth(f, 1, 1))
                    if n < NP:
                        scores_by_key(i, n)
                    if n == 3 and f is not None:
                        if g is not None:
                            pe.wait_ge(d_y3, nth(g, 2, 1))
                        transposed_x2(f)
                    if n in (0, 1, 2, 4) and g is not None:
                        part = n - n // 4
                        layer2(g, part // 2, range(4 * (part % 2), 4 * (part % 2) + 4))
                    if n == 7 and g is not None:
                        pe.wait_ge(d_y3, nth(g, 2, 2))
                    if n == NP and more:
                        pe.wait_ge(a_p, nth(i, NP, NP - 1))
                        transposed_inputs(i + 1)
                    if n >= 5 and f is not None:
                        layer0(f, n - 5)
                    if n >= 1:
                        values(i, n - 1)
                if f is not None:
                    layer0(f, 4)
                    layer0(f, 5)
                if more:
                    pe.wait_ge(a_xt, nth(i + 1, 1, 1))
                    pe.wait_ge(d_xt, nth(i + 1, 1, 1))
                    queries_keys(i + 1, 0)
                if f is not None:
                    layer0(f, 6)
                    layer0(f, 7)
                if more:
                    queries_keys(i + 1, 1)
                    pe.wait_ge(a_ct, nth(i + 1, 1, 1))
                    self_values(i + 1)
                layer1_until(f, 0, Z_PJ)
                pe.wait_ge(a_oh, nth(i, 2, 2))
                pe.wait_ge(d_ol, nth(i, 2, 2))
                for b in range(TB):
                    last = tokens_by_weights(ps[:, 4, b * D:(b + 1) * D], o_h, o_l, b, wp_h, wp_l, slice(0, D))
                last.then_inc(pe_pj, 1)
                layer1_until(f, Z_PJ, Z_LN)
                pe.wait_ge(d_x1, nth(i, 2, 2))
                transposes(x1, 3, i, pe_x1t)
                layer1_until(f, Z_LN, Z_XT)
                pe.wait_ge(a_x1t, nth(i, 1, 1))
                if more:
                    pe.wait_ge(d_qk, nth(i + 1, 4, 4))
                    pe.wait_ge(d_v, nth(i + 1, 1, 1))
                for u in range(5):
                    if u < 4:
                        if u >= 2:
                            pe.wait_ge(d_q2, nth(i, 4, u - 1))
                        for t in (2 * u, 2 * u + 1):
                            last = weights_by_tokens(ps[:, 6 + u % 2, (t % 2) * S:(t % 2 + 1) * S], wq_h, wq_l,
                                                     slice(t * P, (t + 1) * P), xt_h, xt_l,
                                                     (d_x1t, nth(i, 1, 1)) if t == 0 else None)
                        last.then_inc(pe_q2, 1)
                    if u >= 1:
                        layer1_until(f, Z_Q2[u - 1], Z_Q2[u])
                        pe.wait_ge(a_q2, nth(i, 4, u))
                        cross_scores_by_query(i, 2 * u - 2)
                        cross_scores_by_query(i, 2 * u - 1)
                layer1_until(f, Z_Q2[4], Z_MT)
                pe.wait_ge(d_mx2, nth(i, KX, KX))
                for b in range(TB):
                    last = pe.transpose(ps[:, 2, b * P:(b + 1) * P], row_max2[:, b, :], ident[:])
                last.then_inc(pe_mt2, 1)
                layer1_until(f, Z_MT, 4 * KF)
                pe.wait_ge(d_q2, nth(i, 4, 4))
                pe.wait_ge(a_nm2, nth(i, 1, 1))
                if more:
                    pe.wait_ge(q_stacked, nth(i + 1, 64, 64))
                    pe.wait_ge(k_stacked, nth(i + 1, 64, 64))

                heads = iter(range(H))

                def between():
                    h = next(heads)
                    if h < 2 and f is not None:
                        pe.wait_ge(d_r1, nth(f, 4, 3 + h))
                    if more:
                        scores_by_query(i + 1, h)

                for u in range(5):
                    if u < 4:
                        cross_scores_by_key(i, u, between)
                    if u in (1, 2):
                        steps = iter(range(8))
                        cross_values(i, u - 1, lambda: between() if next(steps) in (1, 5) else None)
                    if u in (3, 4):
                        steps = iter(range(8))
                        cross_values(i, u - 1, lambda: cross_keys(i + 1, u - 3, next(steps)) if more else None)
                if more:
                    pe.wait_ge(d_mx, nth(i + 1, 2 * H, 2 * H))
                    cross_values_of(i + 1, 0, 0)
                    cross_values_of(i + 1, 0, 1)
                    cross_values_of(i + 1, 1, 0)
                pe.wait_ge(a_ih, nth(i, 1, 1))
                pe.wait_ge(d_il, nth(i, 1, 1))
                pe.wait_ge(a_o2, nth(i, 4, 4))
                spread_inverse(i, 0)
                spread_inverse(i, 1)
                if more:
                    cross_values_of(i + 1, 1, 1)
                spread_inverse(i, 2)
                spread_inverse(i, 3)
                if more:
                    transposed_max(i + 1)
                for t in range(KX):
                    if t % 2 == 0:
                        pe.wait_ge(a_o2h, nth(i, 4, t // 2 + 1))
                    for n, (a, w) in enumerate(((high, wo_h), (high, wo_l), (low, wo_h))):
                        if t % 2 == 0 and n == 2:
                            pe.wait_ge(d_o2l, nth(i, 4, t // 2 + 1))
                        for b in range(TB):
                            last = pe.matmul(ps[:, 6 + b, 0:D], a[:, t, b * P:(b + 1) * P], w[:, t, :],
                                             start=t == 0 and n == 0, stop=t == KX - 1 and n == 2)
                last.then_inc(pe_wo, 1)

            transposed_inputs(0)
            pe.wait_ge(w_low, 1)
            pe.wait_ge(a_xt, 1)
            pe.wait_ge(d_xt, 1)
            queries_keys(0, 0)
            queries_keys(0, 1)
            pe.wait_ge(a_ct, 1)
            self_values(0)
            pe.wait_ge(d_v, 1)
            pe.wait_ge(wkv_in, 32)
            for step in range(16):
                cross_keys(0, step // 8, step % 8)
            pe.wait_ge(q_stacked, 64)
            pe.wait_ge(k_stacked, 64)
            for h in range(H):
                scores_by_query(0, h)
            pe.wait_ge(d_mx, 2 * H)
            transposed_max(0)
            for n in range(2):
                for kk in range(KD):
                    cross_values_of(0, n, kk)
            pe.wait_ge(w_low, 4)
            pe.wait_ge(w_bin, 5)
            attention(0, None, None)
            attention(1, 0, None)
            with pe.Fori(2, B - 1) as i:
                attention(i, i - 1, i - 2)
            attention(B - 1, B - 2, B - 3, more=False)
            for b in range(TB):
                layer2(B - 2, b)
            pe.wait_ge(d_y3, nth(B - 2, 2, 1))
            transposed_x2(B - 1)
            pe.wait_ge(d_y3, nth(B - 2, 2, 2))
            for m in range(KF):
                layer0(B - 1, m)
            layer1_until(B - 1, 0, 4 * KF)
            for b in range(TB):
                layer2(B - 1, b)


_INS = ["x", "ctx_1024", "L0_attn_w_qkv", "L0_attn_b_qkv", "L0_attn_w_proj", "L0_attn_b_proj", "L0_xattn_w_q",
        "L0_xattn_w_k", "L0_xattn_w_v", "L0_xattn_w_o", "L0_ffn_k0", "L0_ffn_k1", "L0_ffn_k2", "L0_ffn_s0",
        "L0_ffn_s1", "L0_ffn_s2"]


def kernel(**inputs):
    import numpy as _np
    import concourse.bacc as _bacc
    from concourse import mybir as _mybir
    from concourse.bass_utils import run_bass_kernel_spmd as _run

    nc = _bacc.Bacc("TRN2", target_bir_lowering=False, num_devices=1)
    arrays, args = {}, []
    for name in _INS:
        a = _np.ascontiguousarray(inputs[name])
        arrays[f"in_{name}"] = a
        args.append(nc.dram_tensor(f"in_{name}", a.shape, _mybir.dt.from_np(a.dtype), kind="ExternalInput").ap())
    shape = tuple(inputs["x"].shape)
    args.append(nc.dram_tensor("out_0", shape, _mybir.dt.float32, kind="ExternalOutput").ap())
    decoder_layer(nc, *args)
    r = _run(nc, [arrays], core_ids=[0])
    return r.results[0]["out_0"]
```
